# Optimizing a Trainium2 kernel written in Bass

```python
import numpy as np
import jax
import jax.numpy as jnp

def _softmax(x, axis=-1):
    return jax.nn.softmax(x, axis=axis)

def _gelu(x):
    return jax.nn.gelu(x, approximate=True)

def _silu(x):
    return jax.nn.silu(x)

def _sigmoid(x):
    return jax.nn.sigmoid(x)

def _layernorm(x, axis=-1, eps=1e-05):
    m = jnp.mean(x, axis=axis, keepdims=True)
    v = jnp.var(x, axis=axis, keepdims=True)
    return (x - m) / jnp.sqrt(v + eps)

def _scatter_add(tgt, idx, src, axis=0):
    return tgt.at[idx].add(src)

def _segment_sum(src, seg, n):
    return jax.ops.segment_sum(src, seg, n)
kernel_name = 'mk_vit_tower_d1_tok_img1024_r4_3bfeac'

def setup_inputs(seed: int=0):
    np.random.seed(seed)
    _w = jnp.asarray

    def _rec_inputs():
        import jax
        import jax.numpy as jnp
        _rk = jax.random.key(seed)
        x = -7.10856e-05 + 0.999911 * jax.random.normal(jax.random.fold_in(_rk, 1), (16, 4, 128, 256), jnp.float32)
        return x
    x = _rec_inputs()

    def _L0_tok_setup():
        import jax, jax.numpy as jnp
        import numpy as np
        NUM_GROUPS = 4
        IN_CHANNELS = 128
        HIDDEN = IN_CHANNELS // 4
        key = jax.random.key(seed)
        ks = jax.random.split(key, 5)
        B, G, C, D = (32, NUM_GROUPS, IN_CHANNELS, 256)
        x = jax.random.normal(ks[0], (B, G, C, D), dtype=jnp.float32)
        w1 = jax.random.normal(ks[1], (HIDDEN, C), dtype=jnp.float32) / np.sqrt(C)
        b1 = jnp.zeros((HIDDEN,), dtype=jnp.float32)
        w2 = jax.random.normal(ks[2], (C * G, HIDDEN), dtype=jnp.float32) / np.sqrt(HIDDEN)
        b2 = jnp.zeros((C * G,), dtype=jnp.float32)
        return {'x': x, 'w1': w1, 'b1': b1, 'w2': w2, 'b2': b2}
    _L0_tok_all = _L0_tok_setup()
    _L0_tok_in = {k: v for k, v in _L0_tok_all.items() if k in ('w1', 'b1', 'w2', 'b2')}
    del _L0_tok_all

    def _L0_attn_setup():
        import jax, jax.numpy as jnp
        import numpy as np
        from math import sqrt
        NUM_HEADS = 16
        key = jax.random.key(seed)
        ks = jax.random.split(key, 5)
        B, S, H = (2, 512, 256)
        scale = 0.02
        return {'x': jax.random.normal(ks[0], (B, S, H), dtype=jnp.float32), 'W_qkv': jax.random.normal(ks[1], (3 * H, H), dtype=jnp.float32) * scale, 'b_qkv': jax.random.normal(ks[2], (3 * H,), dtype=jnp.float32) * scale, 'W_o': jax.random.normal(ks[3], (H, H), dtype=jnp.float32) * scale, 'b_o': jax.random.normal(ks[4], (H,), dtype=jnp.float32) * scale}
    _L0_attn_all = _L0_attn_setup()
    _L0_attn_in = {k: v for k, v in _L0_attn_all.items() if k in ('W_qkv', 'b_qkv', 'W_o', 'b_o')}
    del _L0_attn_all

    def _L0_ffn_setup():
        import jax, jax.numpy as jnp
        import numpy as np
        from jax import lax
        HIDDEN = 256
        INTER = 128
        E = 64
        K = 6
        G = 8
        TG = 4
        NSH = 2
        ISH = INTER * NSH

        def _moe_forward(hidden_states, gate_w, gate_bias, eg_w, eu_w, ed_w, sg_w, su_w, sd_w):
            B, S, H = hidden_states.shape
            x = hidden_states.reshape(-1, H)
            T = x.shape[0]
            shared = jax.nn.silu(x @ sg_w.T) * (x @ su_w.T) @ sd_w.T
            logits = x @ gate_w.T
            scores = jax.nn.sigmoid(logits) + gate_bias
            group_scores = scores.reshape(T, G, E // G).max(axis=-1)
            _, sel_groups = lax.top_k(group_scores, TG)
            group_mask = jnp.zeros((T, G), scores.dtype).at[jnp.arange(T)[:, None], sel_groups].set(1.0)
            mask = jnp.repeat(group_mask, E // G, axis=1)
            masked_scores = scores * mask
            topk_w, topk_i = lax.top_k(masked_scores, K)
            topk_w = topk_w / (topk_w.sum(axis=-1, keepdims=True) + 1e-08)
            comb = jnp.zeros((T, E), x.dtype).at[jnp.arange(T)[:, None], topk_i].add(topk_w)
            h = jax.nn.silu(jnp.einsum('th,eih->eti', x, eg_w)) * jnp.einsum('th,eih->eti', x, eu_w)
            routed = jnp.einsum('eti,ehi,te->th', h, ed_w, comb)
            return (shared + routed).reshape(B, S, H)
        key = jax.random.key(seed)
        ks = jax.random.split(key, 9)
        s = 0.02
        return {'hidden_states': jax.random.normal(ks[0], (1, 256, HIDDEN), jnp.float32), 'gate_w': jax.random.normal(ks[1], (E, HIDDEN), jnp.float32) * s, 'gate_bias': jnp.zeros((E,), jnp.float32), 'eg_w': jax.random.normal(ks[2], (E, INTER, HIDDEN), jnp.float32) * s, 'eu_w': jax.random.normal(ks[3], (E, INTER, HIDDEN), jnp.float32) * s, 'ed_w': jax.random.normal(ks[4], (E, HIDDEN, INTER), jnp.float32) * s, 'sg_w': jax.random.normal(ks[5], (ISH, HIDDEN), jnp.float32) * s, 'su_w': jax.random.normal(ks[6], (ISH, HIDDEN), jnp.float32) * s, 'sd_w': jax.random.normal(ks[7], (HIDDEN, ISH), jnp.float32) * s}
    _L0_ffn_all = _L0_ffn_setup()
    _L0_ffn_in = {k: v for k, v in _L0_ffn_all.items() if k in ('gate_w', 'gate_bias', 'eg_w', 'eu_w', 'ed_w', 'sg_w', 'su_w', 'sd_w')}
    del _L0_ffn_all
    return {'x': x, 'L0_tok_w1': _L0_tok_in['w1'], 'L0_tok_b1': _L0_tok_in['b1'], 'L0_tok_w2': _L0_tok_in['w2'], 'L0_tok_b2': _L0_tok_in['b2'], 'L0_attn_W_qkv': _L0_attn_in['W_qkv'], 'L0_attn_b_qkv': _L0_attn_in['b_qkv'], 'L0_attn_W_o': _L0_attn_in['W_o'], 'L0_attn_b_o': _L0_attn_in['b_o'], 'L0_ffn_gate_w': _L0_ffn_in['gate_w'], 'L0_ffn_gate_bias': _L0_ffn_in['gate_bias'], 'L0_ffn_eg_w': _L0_ffn_in['eg_w'], 'L0_ffn_eu_w': _L0_ffn_in['eu_w'], 'L0_ffn_ed_w': _L0_ffn_in['ed_w'], 'L0_ffn_sg_w': _L0_ffn_in['sg_w'], 'L0_ffn_su_w': _L0_ffn_in['su_w'], 'L0_ffn_sd_w': _L0_ffn_in['sd_w']}

def reference(x, L0_tok_w1, L0_tok_b1, L0_tok_w2, L0_tok_b2, L0_attn_W_qkv, L0_attn_b_qkv, L0_attn_W_o, L0_attn_b_o, L0_ffn_gate_w, L0_ffn_gate_bias, L0_ffn_eg_w, L0_ffn_eu_w, L0_ffn_ed_w, L0_ffn_sg_w, L0_ffn_su_w, L0_ffn_sd_w):
    import jax
    import jax.numpy as jnp

    def _L0_tok_ref(x, w1, b1, w2, b2):
        import jax, jax.numpy as jnp
        import numpy as np
        NUM_GROUPS = 4
        IN_CHANNELS = 128
        HIDDEN = IN_CHANNELS // 4
        B, G, C, D = x.shape
        w = x.sum(axis=1).mean(axis=2)
        h = jax.nn.gelu(w @ w1.T + b1)
        w = h @ w2.T + b2
        w = w.reshape(B, C, G).transpose(2, 0, 1)
        w = jax.nn.softmax(w, axis=0)
        out = jnp.einsum('bgcd,gbc->bcd', x, w)
        return out

    def _L0_attn_ref(x, W_qkv, b_qkv, W_o, b_o):
        import jax, jax.numpy as jnp
        import numpy as np
        from math import sqrt
        NUM_HEADS = 16
        B, S, H = x.shape
        nh = NUM_HEADS
        hd = H // nh
        qkv = x @ W_qkv.T + b_qkv
        Q, K, V = (qkv[..., :H], qkv[..., H:2 * H], qkv[..., 2 * H:])
        Q = Q.reshape(B, S, nh, hd)
        K = K.reshape(B, S, nh, hd)
        V = V.reshape(B, S, nh, hd)
        scores = jnp.einsum('bqhd,bkhd->bhqk', Q, K)
        causal = jnp.tril(jnp.ones((S, S), dtype=bool))
        scores = jnp.where(causal, scores, -jnp.inf)
        probs = jax.nn.softmax(scores / sqrt(hd), axis=-1)
        out = jnp.einsum('bkhd,bhqk->bqhd', V, probs)
        out = out.reshape(B, S, H)
        return out @ W_o.T + b_o

    def _L0_ffn_ref(hidden_states, gate_w, gate_bias, eg_w, eu_w, ed_w, sg_w, su_w, sd_w):
        import jax, jax.numpy as jnp
        import numpy as np
        from jax import lax
        HIDDEN = 256
        INTER = 128
        E = 64
        K = 6
        G = 8
        TG = 4
        NSH = 2
        ISH = INTER * NSH

        def _moe_forward(hidden_states, gate_w, gate_bias, eg_w, eu_w, ed_w, sg_w, su_w, sd_w):
            B, S, H = hidden_states.shape
            x = hidden_states.reshape(-1, H)
            T = x.shape[0]
            shared = jax.nn.silu(x @ sg_w.T) * (x @ su_w.T) @ sd_w.T
            logits = x @ gate_w.T
            scores = jax.nn.sigmoid(logits) + gate_bias
            group_scores = scores.reshape(T, G, E // G).max(axis=-1)
            _, sel_groups = lax.top_k(group_scores, TG)
            group_mask = jnp.zeros((T, G), scores.dtype).at[jnp.arange(T)[:, None], sel_groups].set(1.0)
            mask = jnp.repeat(group_mask, E // G, axis=1)
            masked_scores = scores * mask
            topk_w, topk_i = lax.top_k(masked_scores, K)
            topk_w = topk_w / (topk_w.sum(axis=-1, keepdims=True) + 1e-08)
            comb = jnp.zeros((T, E), x.dtype).at[jnp.arange(T)[:, None], topk_i].add(topk_w)
            h = jax.nn.silu(jnp.einsum('th,eih->eti', x, eg_w)) * jnp.einsum('th,eih->eti', x, eu_w)
            routed = jnp.einsum('eti,ehi,te->th', h, ed_w, comb)
            return (shared + routed).reshape(B, S, H)
        return _moe_forward(hidden_states, gate_w, gate_bias, eg_w, eu_w, ed_w, sg_w, su_w, sd_w)
    h = _L0_tok_ref(x, L0_tok_w1, L0_tok_b1, L0_tok_w2, L0_tok_b2)
    h = h + _L0_attn_ref(_layernorm(h, axis=-1), L0_attn_W_qkv, L0_attn_b_qkv, L0_attn_W_o, L0_attn_b_o)
    h = h + _L0_ffn_ref(_layernorm(h, axis=-1), L0_ffn_gate_w, L0_ffn_gate_bias, L0_ffn_eg_w, L0_ffn_eu_w, L0_ffn_ed_w, L0_ffn_sg_w, L0_ffn_su_w, L0_ffn_sd_w)
    return h

_drawn_inputs = setup_inputs


def setup_inputs(seed=0):
    import zlib

    import numpy as np

    out = dict(_drawn_inputs(seed))
    spreads = {'L0_tok_b1': (0.0, 0.1), 'L0_tok_b2': (0.0, 0.1), 'L0_ffn_gate_bias': (0.0, 0.787)}
    factors = {'L0_attn_b_qkv': 3.736,
     'L0_ffn_gate_w': 6.736,
     'L0_ffn_eg_w': 5.882,
     'L0_ffn_eu_w': 5.801,
     'L0_ffn_ed_w': 5.799,
     'L0_ffn_sg_w': 4.535,
     'L0_ffn_su_w': 4.487,
     'L0_ffn_sd_w': 4.494}
    for name, (base, spread) in spreads.items():
        noise = np.random.default_rng([zlib.crc32(name.encode()), seed]).standard_normal(out[name].shape)
        drawn = base * np.exp(spread * noise) if base else spread * noise
        out[name] = jnp.asarray(drawn.astype(out[name].dtype))
    for name, factor in factors.items():
        out[name] = (out[name] * factor).astype(out[name].dtype)
    return out
```

```python
import concourse.bass as bass
from concourse import mybir
from contextlib import ExitStack

F32 = mybir.dt.float32
BF16 = mybir.dt.bfloat16
I32 = mybir.dt.int32
ALU = mybir.AluOpType
ACT = mybir.ActivationFunctionType
AX = mybir.AxisListType.X
SP, PE = mybir.EngineType.SP, mybir.EngineType.PE

P = 128
NB = 16
NG = 4
D = 256
KT = D // P
TOKENS = NB * P
HID = 32
HEADS, HD = 16, 16
GH = 4
NGRP = HEADS // GH
E, INTER, TOPK = 64, 128, 6
EG, TOPG = 8, 4
EPS = 1e-5
BIG = 3.0e38
NEG = -1.0e30

REGION = TOKENS + P
SLOTS = E * REGION
ROW = D + 2 * TOPK + 1
W_AT, S_AT, ID_AT = D, D + TOPK, D + 2 * TOPK
NTILES = (TOKENS * TOPK - E) // P + E
U = 8
NT = -(-NTILES // U) * U
RING = 8
NACC = 4
WCOLS = KT * 2 * INTER + D

_at = 0
C_AT = {}
for _name, _n in (("ident", P), ("causal", P), ("before", P), ("head", 8), ("ebase", E), ("ids", NB),
                  ("pad", ROW), ("upto", E), ("tile", NT), ("part", 1)):
    C_AT[_name] = (_at, _n)
    _at += _n
C_COLS = _at


def wait(eng, sem, n):
    if not isinstance(n, int) or n > 0:
        eng.wait_ge(sem, n)


def build(nc, x, w1t, b1, w2t, b2, wqkv, bqk, bv, wo, bo, gate, gbias, sgu, sd, wexp, const, out):
    ds = bass.ds
    slots_dram = nc.dram_tensor("slot_rows", (SLOTS + P, ROW), F32, kind="Internal").ap()
    acc_dram = [nc.dram_tensor(f"acc{a}", (TOKENS + P, D), F32, kind="Internal").ap() for a in range(NACC)]

    with ExitStack() as ctx:
        def sb(name, shape, dt=F32):
            return ctx.enter_context(nc.sbuf_tensor(name, shape, dt))

        def psum(name):
            return ctx.enter_context(nc.psum_tensor(name, [P, 512], F32))

        def sem(name):
            return ctx.enter_context(nc.semaphore(name))

        const_sb = sb("const_sb", [P, C_COLS])

        def c(name, rows=P):
            at, n = C_AT[name]
            return const_sb[0:rows, at:at + n]

        ident = c("ident")
        ident_b = sb("ident_b", [P, P], BF16)
        causal_b = sb("causal_b", [P, GH, P], BF16)
        before_b = sb("before_b", [P, P], BF16)
        ones_b = sb("ones_b", [P, P], BF16)
        upto_b = sb("upto_b", [E, E], BF16)
        ones_f = sb("ones_f", [P, P])
        w1_sb = sb("w1_sb", [P, HID])
        b1_sb = sb("b1_sb", [HID, 1])
        w2_sb = sb("w2_sb", [HID, NG, P])
        b2_sb = sb("b2_sb", [P, NG])
        wqkv_sb = sb("wqkv_sb", [P, KT, 3 * D])
        bqk_sb = sb("bqk_sb", [P, 4])
        bv_sb = sb("bv_sb", [P, D])
        wo_sb = sb("wo_sb", [P, KT, D])
        bo_sb = sb("bo_sb", [P, D])
        gate_sb = sb("gate_sb", [P, KT, E])
        gbias_sb = sb("gbias_sb", [P, E])
        gbias_half = sb("gbias_half", [P, E])
        sgu_sb = sb("sgu_sb", [P, KT, 2 * D])
        sd_sb = sb("sd_sb", [P, KT, D])
        zeros = sb("zeros", [P, 1024])

        x_sb = sb("x_sb", [P, NB, NG, D])
        junk = sb("junk", [P, NG * D])
        xsum = sb("xsum", [P, NB])
        gel = sb("gel", [HID, 5, NB])
        wtok = sb("wtok", [P, NB, NG])
        wsm = sb("wsm", [P, 3, NB])
        wexpd = sb("wexpd", [P, NB, NG])
        wshift = sb("wshift", [P, NB, NG])
        h_all = sb("h_all", [P, NB, D])
        st1 = sb("st1", [P, 6])
        mv1 = sb("mv1", [P, 2])
        rs1 = sb("rs1", [P, 4])
        xn = sb("xn", [P, 2, D])
        xnt = sb("xnt", [P, 2, KT, P])
        qt = sb("qt", [P, 2, 2, P])
        kt = sb("kt", [P, 2, 2, P])
        kmask = sb("kmask", [P, 2, HEADS, P])
        vaug = sb("vaug", [P, 2, HEADS, 2 * HD])
        smax = sb("smax", [P, 2, GH])
        sdif = sb("sdif", [P, 2, GH, P])
        prob = sb("prob", [P, 2, GH, P])
        probt = sb("probt", [P, 2, GH, P])
        ot_sb = sb("ot_sb", [P, NGRP, P])
        rden = sb("rden", [P, HEADS])
        o_sb = sb("o_sb", [P, D])
        ont = sb("ont", [P, KT, P])
        proj = sb("proj", [P, D])
        st2 = sb("st2", [P, 6])
        mv2 = sb("mv2", [P, 2])
        rs2 = sb("rs2", [P, 4])
        row = sb("row", [P, 2, ROW])
        x2t = sb("x2t", [P, KT, P])
        gth = sb("gth", [P, E])
        score = sb("score", [P, E])
        gmx = sb("gmx", [P, EG + TOPG])
        gmx8 = sb("gmx8", [P, 8])
        gmr = sb("gmr", [P, EG + TOPG])
        gsel = sb("gsel", [P, EG])
        masked = sb("masked", [P, 2, E + 2])
        top8 = sb("top8", [P, 8])
        topr = sb("topr", [P, E + 2])
        tsum = sb("tsum", [P, 1])
        tinv = sb("tinv", [P, 2])
        sel_b = sb("sel_b", [P, 2, E], BF16)
        selsum = sb("selsum", [P, E], BF16)
        key0 = sb("key0", [P, E])
        key = sb("key", [P, E])
        key8 = sb("key8", [P, 8])
        wraw = sb("wraw", [P, TOPK])
        wjunk = sb("wjunk", [P, TOPK, E])
        slot_ix = sb("slot_ix", [P, 2, TOPK], I32)
        sth = sb("sth", [P, D])
        sga = sb("sga", [P, D])
        sh = sb("sh", [P, D])
        sht = sb("sht", [P, KT, P])
        acc_sb = sb("acc_sb", [P, 2, D])
        cnt_i = sb("cnt_i", [E, 2], I32)
        nt_f = sb("nt_f", [E, 3])
        nt_b = sb("nt_b", [E, 1], BF16)
        cum = sb("cum", [E, 1])
        past = sb("past", [E, NT])
        pad_ix = sb("pad_ix", [1, E], I32)
        tab = sb("tab", [1, 4, NT])
        tabf = sb("tabf", [1, 4, NT + 1])
        tab_i = sb("tab_i", [1, NT, 4], I32)
        rank_i = sb("rank_i", [1, NT], I32)
        myslot = sb("myslot", [P, NT])
        flat = x_sb[:].rearrange("p b g d -> p (b g d)")
        wring = flat[:, 0:RING * WCOLS].rearrange("p (r n) -> p r n", r=RING)
        xring = flat[:, RING * WCOLS:RING * WCOLS + U * ROW].rearrange("p (r n) -> p r n", r=U)
        xt = sb("xt", [P, 2, KT, P])
        silu = sb("silu", [P, 2, INTER])
        hm = sb("hm", [P, 2, INTER])
        ht = sb("ht", [P, 2, P])
        wtile = sb("wtile", [P, NACC, 1])
        wtj = sb("wtj", [P, NACC, TOPK])
        y = sb("y", [P, NACC, D])

        ps = [psum(f"ps{i}") for i in range(8)]
        psS, psT, psO, psA, psX, psC = ps[0:2], ps[2:4], ps[4], ps[5], ps[6], ps[7]

        s = {}

        def S(name):
            if name not in s:
                s[name] = sem(name)
            return s[name]

        weights_in = [S(f"weights_in{i}") for i in range(15)]
        const_in = S("const_in")
        x_in = [S(f"x_in{i}") for i in range(4)]
        for name in ("consts_ready", "zeros_ready", "sum_act", "sum_dve", "tok_chain", "tok_hid", "tok_tanh", "tok_h",
                     "tok_w", "tok_shift", "tok_exp", "tok_ready",
                     "a_chain", "ln1_done", "xn_transposed", "xnt_ready", "qk_done", "qk_ready", "kmask_ready",
                     "v_done", "v_ready",
                     "scores_done", "max_done", "shift_done", "exp_done", "prob_transposed", "probt_ready",
                     "pv_done", "ot_ready", "ot_turned", "c2_chain", "o_ready", "o_transposed", "ont_ready",
                     "proj_done", "c5_chain", "x2_ready", "x2_transposed", "x2t_ready", "gate_done", "gu_done",
                     "gate_tanh", "gu_tanh", "sh_chain", "sh_ready", "sh_transposed", "sht_ready", "shared_done",
                     "acc0_ready", "g_chain", "sel_ready", "pos_done", "key_read", "d_chain", "row_ready",
                     "t_chain", "t_count", "t_cum", "t_past", "t_rows", "t_rowf", "t_bcast", "tab_ready",
                     "pad_ready", "myslot_ready",
                     "xt_done", "xt_ready", "up_done", "silu_done", "h_ready", "h_turned", "ht_ready",
                     "down_done", "wt_done", "y_ready", "fin_ready"):
            S(name)
        scattered = [S(f"scattered{i}") for i in range(2)]
        acc0_in = [S(f"acc0_in{i}") for i in range(2)]
        acc_zero = S("acc_zero")
        padded = S("padded")
        w_in = [S(f"w_in{q}") for q in range(U)]
        xt_in = [S(f"xt_in{q}") for q in range(U)]
        added = [S(f"added{a}") for a in range(NACC)]
        fin_in = [S(f"fin_in{i}") for i in range(2)]
        fin_out = [S(f"fin_out{i}") for i in range(2)]

        CH = 4 * D
        NCH = TOKENS * D // P // CH
        fin_sb = flat.rearrange("p (i a n) -> p i a n", a=NACC, n=CH)

        block = ctx.enter_context(nc.Block())

        def image_loop(eng, step, first, last):
            for b in range(first, 4):
                step(b, b % 2)
            with eng.Fori(2, 7) as i:
                for par in range(2):
                    step(2 * i + par, par)
            for b in range(14, last + 1):
                step(b, b % 2)

        def has(b, lo=0, hi=NB - 1):
            return not isinstance(b, int) or lo <= b <= hi

        def tile_loop(eng, step, first, last):
            for t in range(first, U):
                step(0, t, t)
            with eng.Fori(1, NT // U - 1) as i:
                for q in range(U):
                    step(i, q, U * i + q)
            for t in range(NT - U, last + 1):
                step(NT // U - 1, t - (NT - U), t)

        def loaded(src, engine, most):
            why = "the table's making bounds it for any counts"
            _, vals = nc.values_load_multi_w_load_instructions(src, engines=[engine], min_val=0, max_val=max(most),
                                                               skip_runtime_bounds_check_because=why)
            return [nc.s_assert_within(v, 0, m, skip_runtime_bounds_check_because=why)
                    for v, m in zip(vals, most)]

        @block.sync
        def _(sp):
            sp.dma_start(const_sb[:], const).then_inc(const_in, 16)
            sp.dma_start(w1_sb[:], w1t).then_inc(weights_in[0], 16)
            sp.dma_start(b1_sb[:], b1).then_inc(weights_in[1], 16)
            for j in range(4):
                sp.dma_start(x_sb[:, 4 * j:4 * j + 4, :, :].rearrange("p b g d -> p (b g) d"),
                             x[4 * j:4 * j + 4].rearrange("b g c d -> c (b g) d")).then_inc(x_in[j], 16)
            sp.dma_start(w2_sb[:], w2t).then_inc(weights_in[2], 16)
            sp.dma_start(b2_sb[:], b2).then_inc(weights_in[3], 16)
            sp.dma_start(wqkv_sb[:], wqkv).then_inc(weights_in[4], 16)
            sp.dma_start(bqk_sb[:], bqk).then_inc(weights_in[5], 16)
            sp.dma_start(bv_sb[:], bv.to_broadcast([P, D])).then_inc(weights_in[6], 16)
            sp.dma_start(wo_sb[:], wo).then_inc(weights_in[7], 16)
            sp.dma_start(bo_sb[:], bo.to_broadcast([P, D])).then_inc(weights_in[8], 16)
            sp.dma_start(gbias_sb[:], gbias.to_broadcast([P, E])).then_inc(weights_in[9], 16)
            sp.dma_start(gate_sb[:], gate).then_inc(weights_in[10], 16)
            sp.dma_start(sgu_sb[:], sgu).then_inc(weights_in[11], 16)
            sp.dma_start(sd_sb[:], sd).then_inc(weights_in[12], 16)
            sp.wait_ge(const_in, 16)
            sp.wait_ge(S("zeros_ready"), 1)
            for a in range(NACC):
                if a:
                    for j in range(4):
                        sp.dma_start(acc_dram[a][j * 512:(j + 1) * 512, :].rearrange("(p n) d -> p (n d)", p=P),
                                     zeros[:]).then_inc(acc_zero, 16)
                sp.dma_start(acc_dram[a][TOKENS:TOKENS + P, :], zeros[:, 0:D]).then_inc(acc_zero, 16)
            sp.dma_start(slots_dram[SLOTS:SLOTS + P, :], c("pad")).then_inc(acc_zero, 16)

            def store_acc0(b, par):
                d = b - 2
                if has(d):
                    sp.wait_ge(S("acc0_ready"), d + 1)
                    sp.dma_start(acc_dram[0][ds(d * P, P), :], acc_sb[:, par, :]).then_inc(acc0_in[par], 16)
            image_loop(sp, store_acc0, 0, NB + 1)

            sp.wait_ge(S("pad_ready"), 1)
            with sp.Fori(0, E) as e:
                at, = loaded(pad_ix[0:1, ds(e, 1)], SP, (SLOTS - P,))
                sp.dma_start(slots_dram[ds(at, P), :], c("pad")).then_inc(padded, 16)
            sp.wait_ge(padded, 16 * E)
            sp.wait_ge(acc_zero, 16 * (NACC * 5 - 4 + 1))
            for par in range(2):
                sp.wait_ge(scattered[par], 16 * TOPK * NB // 2)
                sp.wait_ge(acc0_in[par], 16 * NB // 2)
            sp.wait_ge(S("tab_ready"), 4)

            def load_tile(i, q, t):
                wait(sp, S("down_done"), t - RING + 1)
                at, slot, ex, fresh = loaded(tab_i[0:1, ds(t, 1), :].rearrange("p a b -> p (a b)"), SP,
                                             (SLOTS, RING - 1, E - 1, 1))
                sp.dma_start(wring[:, ds(slot, 1), :], wexp[ds(ex, 1)].rearrange("a p d -> p a d"),
                             cond=fresh).then_inc(w_in[q], 16)
                wait(sp, added[q % NACC], 16 * ((U * i + q - q % NACC) // NACC - 1) if isinstance(i, int)
                     else 16 * (2 * i + q // NACC - 1))
                sp.dma_start(xring[:, q, :], slots_dram[ds(at, P), :]).then_inc(xt_in[q], 16)
            tile_loop(sp, load_tile, 0, NT - 1)

            for a in range(NACC):
                sp.wait_ge(added[a], 16 * (NT // NACC))
            for j in range(NCH):
                for a in range(NACC):
                    sp.dma_start(fin_sb[:, j, a, :], acc_dram[a][j * 4 * P:(j + 1) * 4 * P, :].rearrange(
                        "(p n) d -> p (n d)", p=P)).then_inc(fin_in[j % 2], 16)
                if j:
                    sp.wait_ge(S("fin_ready"), j)
                    sp.dma_start(out[(j - 1) * 4 * P:j * 4 * P, :].rearrange("(p n) d -> p (n d)", p=P),
                                 fin_sb[:, j - 1, 0, :]).then_inc(fin_out[(j - 1) % 2], 16)
            sp.wait_ge(S("fin_ready"), NCH)
            sp.dma_start(out[(NCH - 1) * 4 * P:NCH * 4 * P, :].rearrange("(p n) d -> p (n d)", p=P),
                         fin_sb[:, NCH - 1, 0, :]).then_inc(fin_out[(NCH - 1) % 2], 16)
            for k in range(2):
                sp.wait_ge(fin_out[k], 16 * NCH // 2)

        @block.gpsimd
        def _(pool):
            nc.gpsimd.memset(zeros[:], 0.0).then_inc(S("zeros_ready"), 1)
            pool.wait_ge(const_in, 16)

            def step(b, par):
                d, a = b - 2, b + 1
                if has(d):
                    pool.wait_ge(S("row_ready"), d + 1)
                    pool.sem_inc(S("pool_step"), 1)
                    for k in range(TOPK):
                        nc.gpsimd.indirect_dma_start(
                            out=slots_dram, out_offset=bass.IndirectOffsetOnAxis(ap=slot_ix[:, par, k:k + 1], axis=0),
                            in_=row[:, par, :], in_offset=None).then_inc(scattered[par], 16)
                if has(a):
                    q = 1 - par
                    pool.wait_ge(S("qk_ready"), 4 * a + 4)
                    wait(pool, S("scores_done"), NGRP * (a - 1))
                    for m in range(2):
                        nc.gpsimd.tensor_tensor(
                            kmask[:, q, 8 * m:8 * m + 8, :],
                            kt[:, q, m, :].unsqueeze(1).to_broadcast([P, 8, P]),
                            c("head").unsqueeze(2).to_broadcast([P, 8, P]), ALU.mult).then_inc(S("kmask_ready"), 1)
            image_loop(pool, step, -1, NB + 1)

            def add_tile(i, q, t):
                a = q % NACC
                turn = 2 * i + q // NACC
                pool.wait_ge(S("y_ready"), t + 1)
                wait(pool, added[a], 16 * turn)
                pool.sem_inc(S("pool_step"), 1)
                nc.gpsimd.indirect_dma_start(
                    out=acc_dram[a],
                    out_offset=bass.IndirectOffsetOnAxis(ap=xring[:, q, ID_AT:ID_AT + 1].bitcast(I32), axis=0),
                    in_=y[:, a, :], in_offset=None, compute_op=ALU.add).then_inc(added[a], 16)
            tile_loop(pool, add_tile, 0, NT - 1)

        @block.scalar
        def _(act):
            for j in range(4):
                act.wait_ge(x_in[j], 16)
                for b in range(4 * j, 4 * j + 4, 2):
                    if b:
                        act.wait_ge(S("sum_act"), b // 2)
                    nc.scalar.activation(junk[:], x_sb[:, b, :, :].rearrange("p g d -> p (g d)"), ACT.Identity,
                                         accum_out=xsum[:, b:b + 1]).then_inc(S("sum_act"), 1)
            act.wait_ge(S("tok_hid"), 1)
            nc.scalar.activation(gel[:, 3, :], gel[:, 2, :], ACT.Tanh, scale=0.7978845608028654).then_inc(
                S("tok_tanh"), 1)
            act.wait_ge(S("tok_shift"), 1)
            nc.scalar.activation(wexpd[:], wshift[:], ACT.Exp).then_inc(S("tok_exp"), 1)

            act.wait_ge(weights_in[5], 16)

            def step(b, par):
                a, cc, d = b + 1, b - 1, b - 2
                q = 1 - par

                def exp(g):
                    n, sp = NGRP * b + g, g % 2
                    act.wait_ge(S("shift_done"), n + 1)
                    wait(act, S("prob_transposed"), n - 1)
                    nc.scalar.activation(prob[:, sp], sdif[:, sp], ACT.Exp, scale=HD ** -0.5).then_inc(
                        S("exp_done"), 1)

                def turn(g):
                    n, sp = NGRP * b + g, g % 2
                    act.wait_ge(S("prob_transposed"), n + 1)
                    wait(act, S("pv_done"), n - 1)
                    nc.scalar.copy(probt[:, sp].rearrange("p a k -> p (a k)"), psT[sp][:]).then_inc(
                        S("probt_ready"), 1)

                if has(cc):
                    act.wait_ge(S("pv_done"), NGRP * (cc + 1))
                    wait(act, S("ot_turned"), cc)
                    nc.scalar.copy(ot_sb[:].rearrange("p a k -> p (a k)"), psO[:]).then_inc(S("ot_ready"), 1)
                if has(b):
                    exp(0)
                if has(d):
                    act.wait_ge(S("sh_transposed"), d + 1)
                    wait(act, S("shared_done"), d)
                    nc.scalar.copy(sht[:].rearrange("p a k -> p (a k)"), psC[:, 0:D]).then_inc(S("sht_ready"), 1)
                if has(a):
                    act.wait_ge(S("xn_transposed"), a + 1)
                    wait(act, S("v_done"), a - 1)
                    nc.scalar.copy(xnt[:, q].rearrange("p a k -> p (a k)"), psA[:, 0:D]).then_inc(S("xnt_ready"), 1)
                if has(b):
                    turn(0)
                    exp(1)
                if has(a):
                    act.wait_ge(S("qk_done"), a + 1)
                    wait(act, S("scores_done"), NGRP * (a - 1))
                    wait(act, S("kmask_ready"), 2 * (a - 1))
                    for m in range(4):
                        dst = (qt if m < 2 else kt)[:, q, m % 2, :]
                        nc.scalar.activation(dst, psA[:, m * P:(m + 1) * P], ACT.Identity,
                                             bias=bqk_sb[:, m:m + 1]).then_inc(S("qk_ready"), 1)
                if has(b):
                    turn(1)
                    exp(2)
                if has(cc):
                    act.wait_ge(S("o_transposed"), cc + 1)
                    wait(act, S("proj_done"), cc)
                    nc.scalar.copy(ont[:].rearrange("p a k -> p (a k)"), psC[:, 0:D]).then_inc(S("ont_ready"), 1)
                if has(b):
                    turn(2)
                    exp(3)
                if has(cc):
                    act.wait_ge(S("x2_transposed"), cc + 1)
                    wait(act, S("gu_done"), cc)
                    nc.scalar.copy(x2t[:].rearrange("p a k -> p (a k)"), psX[:, 0:D]).then_inc(S("x2t_ready"), 1)
                if has(b):
                    turn(3)
                if has(cc):
                    act.wait_ge(S("gate_done"), cc + 1)
                    wait(act, S("sel_ready"), cc)
                    nc.scalar.activation(gth[:], psX[:, 0:E], ACT.Tanh, scale=0.5).then_inc(S("gate_tanh"), 1)
                    act.wait_ge(S("gu_done"), cc + 1)
                    wait(act, S("sh_ready"), cc)
                    nc.scalar.activation(sth[:], psC[:, 0:D], ACT.Tanh, scale=0.5).then_inc(S("gu_tanh"), 1)
            image_loop(act, step, -1, NB + 1)

            def tile_step(i, q, t):
                u = t + 1
                if has(u, 0, NT - 1):
                    act.wait_ge(S("xt_done"), u + 1)
                    wait(act, S("up_done"), u - 1)
                    nc.scalar.copy(xt[:, (q + 1) % 2].rearrange("p a k -> p (a k)"),
                                   psT[(q + 1) % 2][:, 0:D]).then_inc(S("xt_ready"), 1)
                if has(t, 0, NT - 1):
                    act.wait_ge(S("up_done"), t + 1)
                    wait(act, S("h_ready"), t - 1)
                    nc.scalar.activation(silu[:, q % 2, :], psS[q % 2][:, 0:INTER], ACT.Silu).then_inc(
                        S("silu_done"), 1)
                if has(t - 1, 0, NT - 1):
                    act.wait_ge(S("h_turned"), t)
                    wait(act, S("down_done"), t - 2)
                    nc.scalar.copy(ht[:, (q + 1) % 2, :], ps[4 + (q + 1) % 2][:, 0:P]).then_inc(S("ht_ready"), 1)
            tile_loop(act, tile_step, -1, NT)

        @block.vector
        def _(dve):
            tok = [0]

            def link(ins, chain, base, count):
                count[0] += 1
                ins.then_inc(S(chain), 1)
                dve.wait_ge(S(chain), base + count[0])

            def start(chain):
                dve.sem_clear(S(chain))
                return [0]

            dve.wait_ge(const_in, 16)
            nc.vector.tensor_copy(ident_b[:], ident)
            for g in range(GH):
                nc.vector.tensor_copy(causal_b[:, g, :], c("causal"))
            nc.vector.tensor_copy(before_b[:], c("before"))
            nc.vector.tensor_copy(upto_b[:], c("upto", E))
            nc.vector.memset(ones_b[:], 1.0)
            nc.vector.memset(ones_f[:], 1.0)
            nc.vector.memset(selsum[:], 0.0)
            nc.vector.memset(gmx[:, EG:], BIG)
            nc.vector.memset(masked[:, :, E:], BIG)
            nc.vector.memset(vaug[:, :, :, HD + 1:], 0.0)
            nc.vector.memset(nt_f[:, 0:1], 1.0)
            nc.vector.memset(tabf[:, 2, 0:1], -1.0)
            nc.vector.memset(vaug[:, :, :, HD:HD + 1], 1.0).then_inc(S("consts_ready"), 1)
            dve.wait_ge(weights_in[9], 16)
            link(nc.vector.tensor_scalar(gbias_half[:], gbias_sb[:], 0.5, None, ALU.add), "tok_chain", 0, tok)

            for j in range(4):
                dve.wait_ge(x_in[j], 16)
                for b in range(4 * j + 1, 4 * j + 4, 2):
                    nc.vector.reduce_sum(xsum[:, b:b + 1], x_sb[:, b, :, :].rearrange("p g d -> p (g d)"),
                                         axis=AX).then_inc(S("sum_dve"), 1)
            dve.wait_ge(weights_in[1], 16)
            dve.wait_ge(S("tok_h"), 1)
            link(nc.vector.tensor_scalar(gel[:, 0, :], psA[0:HID, 0:NB], 1.0 / D, b1_sb[:, 0:1], ALU.mult, ALU.add),
                 "tok_chain", 0, tok)
            link(nc.vector.tensor_tensor(gel[:, 1, :], gel[:, 0, :], gel[:, 0, :], ALU.mult), "tok_chain", 0, tok)
            link(nc.vector.tensor_scalar(gel[:, 1, :], gel[:, 1, :], 0.044715, 1.0, ALU.mult, ALU.add),
                 "tok_chain", 0, tok)
            nc.vector.tensor_tensor(gel[:, 2, :], gel[:, 0, :], gel[:, 1, :], ALU.mult).then_inc(S("tok_hid"), 1)
            dve.wait_ge(S("tok_tanh"), 1)
            nc.vector.scalar_tensor_tensor(out=gel[:, 4, :], in0=gel[:, 3, :], scalar=1.0, in1=gel[:, 0, :],
                                           op0=ALU.add, op1=ALU.mult).then_inc(S("tok_hid"), 1)
            dve.wait_ge(S("tok_w"), 1)
            dve.wait_ge(weights_in[3], 16)
            link(nc.vector.scalar_tensor_tensor(
                out=wtok[:], in0=psA[:, 0:NG * NB].rearrange("p (g b) -> p b g", g=NG), scalar=0.5,
                in1=b2_sb[:].unsqueeze(1).to_broadcast([P, NB, NG]), op0=ALU.mult, op1=ALU.add),
                "tok_chain", 0, tok)
            link(nc.vector.tensor_reduce(wsm[:, 0, :], wtok[:], axis=AX, op=ALU.max), "tok_chain", 0, tok)
            nc.vector.tensor_tensor(wshift[:], wtok[:], wsm[:, 0, :].unsqueeze(2).to_broadcast([P, NB, NG]),
                                    ALU.subtract).then_inc(S("tok_shift"), 1)
            dve.wait_ge(S("tok_exp"), 1)
            link(nc.vector.tensor_reduce(wsm[:, 1, :], wexpd[:], axis=AX, op=ALU.add), "tok_chain", 0, tok)
            link(nc.vector.reciprocal(wsm[:, 2, :], wsm[:, 1, :]), "tok_chain", 0, tok)
            link(nc.vector.tensor_tensor(wtok[:], wexpd[:], wsm[:, 2, :].unsqueeze(2).to_broadcast([P, NB, NG]),
                                         ALU.mult), "tok_chain", 0, tok)

            def norm(free, src, dst, st, mv, rs, chain, base, n, done):
                link(nc.vector.bn_stats(st[:], src), chain, base, n)
                link(nc.vector.bn_aggr(mv[:], st[:]), chain, base, n)
                v, y, r, z = rs[:, 0:1], rs[:, 1:2], rs[:, 2:3], rs[:, 3:4]
                link(nc.vector.tensor_scalar(v, mv[:, 1:2], EPS, None, ALU.add), chain, base, n)
                link(nc.vector.tensor_single_scalar(z.bitcast(I32), v.bitcast(I32), 1, ALU.arith_shift_right),
                     chain, base, n)
                link(nc.vector.tensor_scalar(y.bitcast(I32), z.bitcast(I32), -1.0, float(0x5F3759DF), ALU.mult,
                                             ALU.add), chain, base, n)
                link(nc.vector.scalar_tensor_tensor(out=r, in0=y, scalar=v, in1=y, op0=ALU.mult, op1=ALU.mult),
                     chain, base, n)
                link(nc.vector.tensor_scalar(z, r, 0.375, -1.25, ALU.mult, ALU.add), chain, base, n)
                link(nc.vector.tensor_tensor(z, z, r, ALU.mult), chain, base, n)
                link(nc.vector.scalar_tensor_tensor(out=y, in0=z, scalar=1.875, in1=y, op0=ALU.add, op1=ALU.mult),
                     chain, base, n)
                link(nc.vector.scalar_tensor_tensor(out=r, in0=y, scalar=v, in1=y, op0=ALU.mult, op1=ALU.mult),
                     chain, base, n)
                link(nc.vector.tensor_scalar(z, r, -0.5, 1.5, ALU.mult, ALU.add), chain, base, n)
                link(nc.vector.tensor_tensor(y, y, z, ALU.mult), chain, base, n)
                free()
                nc.vector.tensor_scalar(dst, src, mv[:, 0:1], y, ALU.subtract, ALU.mult).then_inc(
                    S(done), 1)

            def mix_norm(a, q):
                n, base = start("a_chain"), 0
                hb = h_all[:, ds(a, 1), :].rearrange("p a d -> p (a d)")

                def xg(g):
                    return x_sb[:, ds(a, 1), g, :].rearrange("p a d -> p (a d)")

                def wg(g):
                    return wtok[:, ds(a, 1), g:g + 1].rearrange("p a d -> p (a d)")
                link(nc.vector.tensor_scalar(hb, xg(0), wg(0), None, ALU.mult), "a_chain", base, n)
                for g in range(1, NG):
                    link(nc.vector.scalar_tensor_tensor(out=hb, in0=xg(g), scalar=wg(g), in1=hb, op0=ALU.mult,
                                                        op1=ALU.add), "a_chain", base, n)
                norm(lambda: wait(dve, S("xn_transposed"), a - 1), hb, xn[:, q, :], st1, mv1, rs1, "a_chain", base, n, "ln1_done")

            def softmax_shift(b, g):
                n, sp = NGRP * b + g, g % 2
                s3 = psS[sp][:].rearrange("p (a k) -> p a k", a=GH)
                dve.wait_ge(S("scores_done"), n + 1)
                nc.vector.tensor_reduce(smax[:, sp, :], s3, axis=AX, op=ALU.max).then_inc(S("max_done"), 1)
                dve.wait_ge(S("max_done"), n + 1)
                wait(dve, S("exp_done"), n - 1)
                nc.vector.tensor_tensor(sdif[:, sp], s3, smax[:, sp, :].unsqueeze(2).to_broadcast([P, GH, P]),
                                        ALU.subtract).then_inc(S("shift_done"), 1)

            def v_evac(a, q):
                dve.wait_ge(S("v_done"), a + 1)
                wait(dve, S("pv_done"), NGRP * (a - 1))
                nc.vector.tensor_tensor(vaug[:, q, :, 0:HD], psA[:, 0:D].rearrange("p (h d) -> p h d", d=HD),
                                        bv_sb[:].rearrange("p (h d) -> p h d", d=HD), ALU.add).then_inc(
                    S("v_ready"), 1)

            def normalise(cc):
                o3 = psX[:].rearrange("p (h d) -> p h d", d=2 * HD)
                dve.wait_ge(S("ot_turned"), cc + 1)
                nc.vector.reciprocal(rden[:], o3[:, :, HD:HD + 1].rearrange("p h o -> p (h o)")).then_inc(
                    S("c2_chain"), 1)
                dve.wait_ge(S("c2_chain"), cc + 1)
                wait(dve, S("o_transposed"), cc)
                nc.vector.tensor_tensor(o_sb[:].rearrange("p (h d) -> p h d", d=HD), o3[:, :, 0:HD],
                                        rden[:].unsqueeze(2).to_broadcast([P, HEADS, HD]), ALU.mult).then_inc(
                    S("o_ready"), 1)

            def residual_norm(cc, q):
                n, base = start("c5_chain"), 0
                hb = h_all[:, ds(cc, 1), :].rearrange("p a d -> p (a d)")
                dve.wait_ge(S("proj_done"), cc + 1)
                link(nc.vector.tensor_tensor(proj[:], psC[:, D:2 * D], bo_sb[:], ALU.add), "c5_chain", base, n)
                link(nc.vector.tensor_tensor(hb, hb, proj[:], ALU.add), "c5_chain", base, n)
                norm(lambda: wait(dve, scattered[q], 8 * TOPK * (cc - q)), hb, row[:, q, 0:D], st2, mv2, rs2, "c5_chain", base, n, "x2_ready")

            def shared_act(cc):
                dve.wait_ge(S("gu_tanh"), cc + 1)
                nc.vector.scalar_tensor_tensor(out=sga[:], in0=sth[:], scalar=1.0, in1=psC[:, 0:D], op0=ALU.add,
                                               op1=ALU.mult).then_inc(S("sh_chain"), 1)
                dve.wait_ge(S("sh_chain"), cc + 1)
                wait(dve, S("sh_transposed"), cc)
                nc.vector.scalar_tensor_tensor(out=sh[:], in0=sga[:], scalar=0.5, in1=psC[:, D:2 * D],
                                               op0=ALU.mult, op1=ALU.mult).then_inc(S("sh_ready"), 1)

            def route(cc, q):
                n, base = start("g_chain"), 0

                def lk(ins):
                    link(ins, "g_chain", base, n)
                dve.wait_ge(S("gate_tanh"), cc + 1)
                lk(nc.vector.scalar_tensor_tensor(out=score[:], in0=gth[:], scalar=0.5, in1=gbias_half[:],
                                                  op0=ALU.mult, op1=ALU.add))
                lk(nc.vector.tensor_reduce(gmx[:, 0:EG], score[:].rearrange("p (g e) -> p g e", g=EG), axis=AX,
                                           op=ALU.max))
                lk(nc.vector.max(gmx8[:], gmx[:]))
                lk(nc.vector.match_replace(gmr[:], gmx8[:], gmx[:], -BIG))
                lk(nc.vector.tensor_scalar(gsel[:], gmr[:, 0:EG], -BIG, None, ALU.is_equal))
                mk = masked[:, q, :]
                lk(nc.vector.tensor_tensor(mk[:, 0:E].rearrange("p (g e) -> p g e", g=EG),
                                           score[:].rearrange("p (g e) -> p g e", g=EG),
                                           gsel[:].unsqueeze(2).to_broadcast([P, EG, EG]), ALU.mult))
                lk(nc.vector.max(top8[:], mk))
                lk(nc.vector.match_replace(topr[:], top8[:], mk, -BIG))
                lk(nc.vector.reduce_sum(tsum[:], top8[:, 2:8], axis=AX))
                lk(nc.vector.tensor_scalar(tsum[:], tsum[:], 1e-8, None, ALU.add))
                lk(nc.vector.reciprocal(tinv[:, q:q + 1], tsum[:]))
                lk(nc.vector.tensor_scalar(sel_b[:, q, :], topr[:, 0:E], -BIG, None, ALU.is_equal))
                nc.vector.tensor_copy(row[:, q, ID_AT:ID_AT + 1].bitcast(I32),
                                      c("ids")[:, ds(cc, 1)].bitcast(I32)).then_inc(S("sel_ready"), 1)

            def place(d, q):
                n, base = start("d_chain"), 0

                def lk(ins):
                    link(ins, "d_chain", base, n)
                dve.wait_ge(S("pos_done"), d + 1)
                nc.vector.tensor_tensor(key0[:], psX[:, 0:E], c("ebase"), ALU.add).then_inc(S("key_read"), 1)
                lk(nc.vector.tensor_tensor(selsum[:], selsum[:], sel_b[:, q, :], ALU.add))
                dve.wait_ge(S("key_read"), d + 1)
                lk(nc.vector.tensor_tensor(key[:], key0[:], sel_b[:, q, :], ALU.mult))
                lk(nc.vector.max(key8[:], key[:]))
                nc.vector.tensor_scalar(slot_ix[:, q, :], key8[:, 0:TOPK], 1.0, None, ALU.subtract)
                nc.vector.tensor_scalar(row[:, q, S_AT:S_AT + TOPK], key8[:, 0:TOPK], 1.0, None, ALU.subtract)
                for k in range(TOPK):
                    lk(nc.vector.scalar_tensor_tensor(
                        out=wjunk[:, k, :], in0=key[:], scalar=key8[:, k:k + 1], in1=masked[:, q, 0:E],
                        op0=ALU.is_equal, op1=ALU.mult, accum_out=wraw[:, k:k + 1]))
                nc.vector.tensor_scalar(row[:, q, W_AT:W_AT + TOPK], wraw[:], tinv[:, q:q + 1], None,
                                        ALU.mult).then_inc(S("row_ready"), 1)

            def acc0(d, q):
                dve.wait_ge(S("shared_done"), d + 1)
                wait(dve, acc0_in[q], 8 * (d - q))
                nc.vector.tensor_tensor(acc_sb[:, q, :], psC[:, D:2 * D],
                                        h_all[:, ds(d, 1), :].rearrange("p a d -> p (a d)"), ALU.add).then_inc(
                    S("acc0_ready"), 1)

            dve.wait_ge(weights_in[6], 16)
            dve.wait_ge(weights_in[8], 16)
            mix_norm(0, 0)

            def step(b, par):
                q = 1 - par
                if has(b):
                    softmax_shift(b, 0)
                if has(b - 2):
                    place(b - 2, par)
                if has(b):
                    softmax_shift(b, 1)
                if has(b - 2):
                    acc0(b - 2, par)
                if has(b - 1):
                    normalise(b - 1)
                if has(b):
                    softmax_shift(b, 2)
                if has(b + 1):
                    v_evac(b + 1, q)
                if has(b - 1):
                    residual_norm(b - 1, q)
                if has(b):
                    softmax_shift(b, 3)
                if has(b + 2):
                    mix_norm(b + 2, par)
                if has(b - 1):
                    shared_act(b - 1)
                    route(b - 1, q)
            image_loop(dve, step, -1, NB + 1)

            tn = [0]

            def lt(ins):
                link(ins, "t_chain", 0, tn)
            dve.wait_ge(S("t_count"), 1)
            lt(nc.vector.tensor_scalar(cnt_i[:, 0:1], psX[0:E, 0:1], float(P - 1), None, ALU.add))
            lt(nc.vector.tensor_single_scalar(cnt_i[:, 1:2], cnt_i[:, 0:1], 7, ALU.arith_shift_right))
            lt(nc.vector.tensor_copy(nt_f[:, 1:2], cnt_i[:, 1:2]))
            nc.vector.tensor_scalar(nt_f[:, 2:3], nt_f[:, 1:2], 0.0, None, ALU.is_gt)
            lt(nc.vector.scalar_tensor_tensor(out=tab[:, 0, 0:E], in0=psX[0:1, E:2 * E], scalar=-1.0,
                                              in1=c("ebase", 1), op0=ALU.add, op1=ALU.add))
            nc.vector.tensor_copy(pad_ix[:], tab[:, 0, 0:E]).then_inc(S("pad_ready"), 1)
            nc.vector.tensor_copy(nt_b[:], nt_f[:, 1:2]).then_inc(S("t_rows"), 1)
            dve.wait_ge(S("t_cum"), 1)
            lt(nc.vector.tensor_copy(cum[:], psX[0:E, 0:1]))
            nc.vector.tensor_scalar(past[:], c("tile", E), cum[:, 0:1], None, ALU.is_ge).then_inc(S("t_rows"), 1)
            dve.wait_ge(S("t_past"), 1)
            ex, before, rank = (psX[0:1, k * NT:(k + 1) * NT] for k in range(3))
            lt(nc.vector.tensor_tensor(tab[:, 1, :], c("tile", 1), before, ALU.subtract))
            lt(nc.vector.tensor_scalar(tab[:, 1, :], tab[:, 1, :], float(P), None, ALU.mult))
            lt(nc.vector.scalar_tensor_tensor(out=tab[:, 2, :], in0=ex, scalar=float(REGION), in1=tab[:, 1, :],
                                              op0=ALU.mult, op1=ALU.add))
            nc.vector.tensor_scalar(tab[:, 3, :], tab[:, 2, :], float(SLOTS), None, ALU.min).then_inc(
                S("t_rowf"), 1)
            dve.wait_ge(S("t_rowf"), 1)
            nc.vector.tensor_copy(tab_i[:, :, 0], tab[:, 3, :]).then_inc(S("tab_ready"), 1)
            nc.vector.tensor_scalar(tab_i[:, :, 2], ex, float(E - 1), None, ALU.min).then_inc(S("tab_ready"), 1)
            lt(nc.vector.tensor_copy(rank_i[:], rank))
            lt(nc.vector.tensor_copy(tabf[:, 2, 1:NT + 1], rank))
            nc.vector.tensor_single_scalar(tab_i[:, :, 1], rank_i[:], RING - 1, ALU.bitwise_and).then_inc(
                S("tab_ready"), 1)
            nc.vector.tensor_tensor(tab_i[:, :, 3], tabf[:, 2, 1:NT + 1], tabf[:, 2, 0:NT],
                                    ALU.not_equal).then_inc(S("tab_ready"), 1)
            dve.wait_ge(S("t_bcast"), 1)
            nc.vector.tensor_scalar(myslot[:], psC[:, 0:NT], c("part"), None, ALU.add).then_inc(
                S("myslot_ready"), 1)
            dve.wait_ge(S("myslot_ready"), 1)

            def tile_step(i, q, t):
                if has(t, 0, NT - 1):
                    dve.wait_ge(xt_in[q], 16 * i + 16)
                    wait(dve, S("y_ready"), t - NACC + 1)
                    nc.vector.scalar_tensor_tensor(
                        out=wtj[:, q % NACC, :], in0=xring[:, q, S_AT:S_AT + TOPK], scalar=myslot[:, ds(t, 1)],
                        in1=xring[:, q, W_AT:W_AT + TOPK], op0=ALU.is_equal, op1=ALU.mult,
                        accum_out=wtile[:, q % NACC, :]).then_inc(S("wt_done"), 1)
                    dve.wait_ge(S("silu_done"), t + 1)
                    wait(dve, S("h_turned"), t - 1)
                    nc.vector.tensor_tensor(hm[:, q % 2, :], silu[:, q % 2, :], psS[q % 2][:, INTER:2 * INTER],
                                            ALU.mult).then_inc(S("h_ready"), 1)
                v, a = t - 2, (q - 2) % NACC
                if has(v, 0, NT - 1):
                    dve.wait_ge(S("down_done"), t - 1)
                    dve.wait_ge(S("wt_done"), t - 1)
                    turn = (2 * i + (q - 2) // NACC)
                    wait(dve, added[a], 16 * turn)
                    nc.vector.tensor_scalar(y[:, a, :], ps[6 + q % 2][:, 0:D], wtile[:, a, :], None,
                                            ALU.mult).then_inc(S("y_ready"), 1)
            tile_loop(dve, tile_step, 0, NT + 1)

            fch = [0]
            for j in range(NCH):
                dve.wait_ge(fin_in[j % 2], 16 * NACC * (j // 2 + 1))
                nc.vector.tensor_tensor(fin_sb[:, j, 0, :], fin_sb[:, j, 0, :], fin_sb[:, j, 1, :], ALU.add)
                link(nc.vector.tensor_tensor(fin_sb[:, j, 2, :], fin_sb[:, j, 2, :], fin_sb[:, j, 3, :], ALU.add),
                     "t_chain", tn[0], fch)
                nc.vector.tensor_tensor(fin_sb[:, j, 0, :], fin_sb[:, j, 0, :], fin_sb[:, j, 2, :],
                                        ALU.add).then_inc(S("fin_ready"), 1)

        @block.tensor
        def _(pe):
            def mm(*a, **k):
                return nc.tensor.matmul(*a, **k)

            def both(dst, lhs, rhs):
                for k in range(KT):
                    last = mm(dst, lhs(k), rhs(k), start=k == 0, stop=k == KT - 1)
                return last

            pe.wait_ge(weights_in[0], 16)
            pe.wait_ge(S("sum_act"), NB // 2)
            pe.wait_ge(S("sum_dve"), NB // 2)
            mm(psA[0:HID, 0:NB], w1_sb[:], xsum[:], start=True, stop=True).then_inc(S("tok_h"), 1)
            pe.wait_ge(weights_in[2], 16)
            pe.wait_ge(S("tok_hid"), 2)
            for g in range(NG):
                last = mm(psA[:, g * NB:(g + 1) * NB], w2_sb[:, g, :], gel[:, 4, :], start=True, stop=True)
            last.then_inc(S("tok_w"), 1)
            for k in (4, 7, 10, 11, 12):
                pe.wait_ge(weights_in[k], 16)
            pe.wait_ge(S("consts_ready"), 1)

            def step(b, par):
                a, cc, d, q = b + 1, b - 1, b - 2, 1 - par

                def scores(g):
                    n, sp = NGRP * b + g, g % 2
                    pe.wait_ge(S("kmask_ready"), 2 * b + 2)
                    wait(pe, S("shift_done"), n - 1)
                    mm(psS[sp][:], ident_b[:], causal_b[:].rearrange("p a k -> p (a k)"), start=True, stop=False)
                    mm(psS[sp][:], qt[:, par, g // 2, :],
                       kmask[:, par, GH * g:GH * g + GH, :].rearrange("p a k -> p (a k)"),
                       start=False, stop=True).then_inc(S("scores_done"), 1)

                def turn(g):
                    n, sp = NGRP * b + g, g % 2
                    pe.wait_ge(S("exp_done"), n + 1)
                    wait(pe, S("probt_ready"), n - 1)
                    for j in range(GH):
                        last = nc.tensor.transpose(psT[sp][:, j * P:(j + 1) * P], prob[:, sp, j, :], ident)
                    last.then_inc(S("prob_transposed"), 1)

                def pv(g):
                    n, sp = NGRP * b + g, g % 2
                    pe.wait_ge(S("probt_ready"), n + 1)
                    pe.wait_ge(S("v_ready"), b + 1)
                    wait(pe, S("ot_ready"), b)
                    for j in range(GH):
                        last = mm(psO[32 * j:32 * j + 32, g * P:(g + 1) * P], vaug[:, par, GH * g + j, :],
                                  probt[:, sp, j, :], start=True, stop=True)
                    last.then_inc(S("pv_done"), 1)

                def two(dst, src, done):
                    for k in range(KT):
                        last = nc.tensor.transpose(dst[:, k * P:(k + 1) * P], src[:, k * P:(k + 1) * P], ident)
                    last.then_inc(S(done), 1)

                if has(b):
                    scores(0)
                if has(d):
                    pe.wait_ge(S("sel_ready"), d + 1)
                    mm(psX[:, 0:E], before_b[:], sel_b[:, par, :], start=True, stop=False)
                    mm(psX[:, 0:E], ones_b[:], selsum[:], start=False, stop=True).then_inc(S("pos_done"), 1)
                    pe.wait_ge(S("sh_ready"), d + 1)
                    two(psC, sh, "sh_transposed")
                if has(a):
                    pe.wait_ge(S("ln1_done"), a + 1)
                    wait(pe, S("v_ready"), a)
                    two(psA, xn[:, q, :], "xn_transposed")
                if has(b):
                    scores(1)
                    turn(0)
                if has(d):
                    pe.wait_ge(S("sht_ready"), d + 1)
                    both(psC[:, D:2 * D], lambda k: sht[:, k, :], lambda k: sd_sb[:, k, :]).then_inc(
                        S("shared_done"), 1)
                if has(cc):
                    pe.wait_ge(S("ot_ready"), cc + 1)
                    wait(pe, S("key_read"), cc)
                    for g in range(NGRP):
                        last = nc.tensor.transpose(psX[:, g * P:(g + 1) * P], ot_sb[:, g, :], ident)
                    last.then_inc(S("ot_turned"), 1)
                if has(b):
                    pv(0)
                if has(a):
                    pe.wait_ge(S("xnt_ready"), a + 1)
                    for m in range(4):
                        last = both(psA[:, m * P:(m + 1) * P], lambda k: wqkv_sb[:, k, m * P:(m + 1) * P],
                                    lambda k: xnt[:, q, k, :])
                    last.then_inc(S("qk_done"), 1)
                if has(b):
                    scores(2)
                    turn(1)
                if has(cc):
                    pe.wait_ge(S("o_ready"), cc + 1)
                    wait(pe, S("acc0_ready"), cc)
                    two(psC, o_sb, "o_transposed")
                if has(b):
                    pv(1)
                if has(a):
                    pe.wait_ge(S("qk_ready"), 4 * a + 4)
                    both(psA[:, 0:D], lambda k: xnt[:, q, k, :], lambda k: wqkv_sb[:, k, 2 * D:3 * D]).then_inc(
                        S("v_done"), 1)
                if has(b):
                    scores(3)
                    turn(2)
                if has(cc):
                    pe.wait_ge(S("ont_ready"), cc + 1)
                    both(psC[:, D:2 * D], lambda k: ont[:, k, :], lambda k: wo_sb[:, k, :]).then_inc(
                        S("proj_done"), 1)
                if has(b):
                    pv(2)
                if has(cc):
                    pe.wait_ge(S("x2_ready"), cc + 1)
                    two(psX, row[:, q, :], "x2_transposed")
                if has(b):
                    turn(3)
                if has(cc):
                    pe.wait_ge(S("x2t_ready"), cc + 1)
                    both(psX[:, 0:E], lambda k: x2t[:, k, :], lambda k: gate_sb[:, k, :]).then_inc(
                        S("gate_done"), 1)
                    both(psC[:], lambda k: x2t[:, k, :], lambda k: sgu_sb[:, k, :]).then_inc(S("gu_done"), 1)
                if has(b):
                    pv(3)
            image_loop(pe, step, -1, NB + 1)

            pe.wait_ge(S("row_ready"), NB)
            mm(psX[0:E, 0:1], selsum[:], ones_b[:, 0:1], start=True, stop=True)
            mm(psX[0:1, E:2 * E], ones_b[:, 0:1], selsum[:], start=True, stop=True).then_inc(S("t_count"), 1)
            pe.wait_ge(S("t_rows"), 1)
            mm(psX[0:E, 0:1], upto_b[:], nt_b[:], start=True, stop=True).then_inc(S("t_cum"), 1)
            pe.wait_ge(S("t_rows"), 2)
            for k in range(3):
                last = mm(psX[0:1, k * NT:(k + 1) * NT], nt_f[:, k:k + 1], past[:], start=True, stop=True)
            last.then_inc(S("t_past"), 1)
            pe.wait_ge(S("t_rowf"), 1)
            mm(psC[:, 0:NT], ones_f[0:1, :], tab[:, 3, :], start=True, stop=True).then_inc(S("t_bcast"), 1)
            pe.wait_ge(S("tab_ready"), 4)
            pe.wait_ge(S("myslot_ready"), 1)

            def tile_step(i, q, t):
                u = t + 1
                if has(u, 0, NT - 1):
                    uq = (q + 1) % U
                    turn = i if q < U - 1 else i + 1
                    if isinstance(i, int) and t == -1:
                        turn = 0
                    pe.wait_ge(xt_in[uq], 16 * turn + 16)
                    wait(pe, S("xt_ready"), u - 1)
                    for k in range(KT):
                        last = nc.tensor.transpose(psT[uq % 2][:, k * P:(k + 1) * P],
                                                   xring[:, uq, k * P:(k + 1) * P], ident)
                    last.then_inc(S("xt_done"), 1)
                if has(t, 0, NT - 1):
                    slot, = loaded(tab_i[0:1, ds(t, 1), 1:2].rearrange("p a b -> p (a b)"), PE, (RING - 1,))
                    pe.wait_ge(S("xt_ready"), t + 1)
                    pe.wait_ge(w_in[q], 16 * i + 16)
                    wait(pe, S("h_ready"), t - 1)
                    both(psS[q % 2][:, 0:2 * INTER], lambda k: xt[:, q % 2, k, :],
                         lambda k: wring[:, ds(slot, 1), k * 2 * INTER:(k + 1) * 2 * INTER]).then_inc(
                        S("up_done"), 1)
                v = t - 1
                if has(v, 0, NT - 1):
                    vq = (q - 1) % 2
                    pe.wait_ge(S("h_ready"), v + 1)
                    wait(pe, S("ht_ready"), v - 1)
                    nc.tensor.transpose(ps[4 + vq][:, 0:P], hm[:, vq, :], ident).then_inc(S("h_turned"), 1)
                v = t - 2
                if has(v, 0, NT - 1):
                    vq = q % 2
                    slot, = loaded(tab_i[0:1, ds(v, 1), 1:2].rearrange("p a b -> p (a b)"), PE, (RING - 1,))
                    pe.wait_ge(S("ht_ready"), v + 1)
                    wait(pe, S("y_ready"), v - 1)
                    mm(ps[6 + vq][:, 0:D], ht[:, vq, :], wring[:, ds(slot, 1), KT * 2 * INTER:WCOLS],
                       start=True, stop=True).then_inc(S("down_done"), 1)
            tile_loop(pe, tile_step, -1, NT + 1)


_ARGS = ("x", "w1t", "b1", "w2t", "b2", "wqkv", "bqk", "bv", "wo", "bo", "gate", "gbias", "sgu", "sd", "wexp",
         "const")


def kernel(x, L0_tok_w1, L0_tok_b1, L0_tok_w2, L0_tok_b2, L0_attn_W_qkv, L0_attn_b_qkv, L0_attn_W_o, L0_attn_b_o,
           L0_ffn_gate_w, L0_ffn_gate_bias, L0_ffn_eg_w, L0_ffn_eu_w, L0_ffn_ed_w, L0_ffn_sg_w, L0_ffn_su_w,
           L0_ffn_sd_w):
    import numpy as np
    import concourse.bacc as bacc
    from concourse.bass_utils import run_bass_kernel_spmd

    def rows(w):
        w = np.asarray(w)
        return np.ascontiguousarray(w.T.reshape(KT, P, w.shape[0]).transpose(1, 0, 2))

    const = np.zeros((P, C_COLS), np.float32)

    def put(name, v):
        at, n = C_AT[name]
        const[:, at:at + n] = v
    p = np.arange(P)
    put("ident", np.eye(P))
    put("causal", np.where(p[None, :] > p[:, None], NEG, 0.0))
    put("before", p[:, None] < p[None, :])
    put("head", p[:, None] // HD == np.arange(8)[None, :])
    put("ebase", np.arange(E)[None, :] * REGION + 1)
    put("ids", (np.arange(NB)[None, :] * P + p[:, None]).astype(np.int32).view(np.float32))
    pad = np.zeros((P, ROW), np.float32)
    pad[:, S_AT:S_AT + TOPK] = -1.0
    pad[:, ID_AT] = (TOKENS + p).astype(np.int32).view(np.float32)
    put("pad", pad)
    put("upto", p[:, None] <= np.arange(E)[None, :])
    put("tile", np.arange(NT)[None, :])
    put("part", p[:, None])

    eg, eu, ed = (np.asarray(w) for w in (L0_ffn_eg_w, L0_ffn_eu_w, L0_ffn_ed_w))
    up = np.stack([eg, eu], 1).reshape(E, 2 * INTER, KT, P).transpose(0, 3, 2, 1).reshape(E, P, KT * 2 * INTER)
    wexp = np.ascontiguousarray(np.concatenate([up, ed.transpose(0, 2, 1)], 2))
    bqkv = np.asarray(L0_attn_b_qkv)
    arrays = dict(
        x=np.asarray(x), w1t=np.ascontiguousarray(np.asarray(L0_tok_w1).T), b1=np.asarray(L0_tok_b1)[:, None],
        w2t=np.ascontiguousarray(np.asarray(L0_tok_w2).reshape(P, NG, HID).transpose(2, 1, 0)),
        b2=np.asarray(L0_tok_b2).reshape(P, NG), wqkv=rows(L0_attn_W_qkv),
        bqk=np.ascontiguousarray(bqkv[:2 * D].reshape(4, P).T), bv=bqkv[2 * D:][None, :], wo=rows(L0_attn_W_o),
        bo=np.asarray(L0_attn_b_o)[None, :], gate=rows(L0_ffn_gate_w), gbias=np.asarray(L0_ffn_gate_bias)[None, :],
        sgu=rows(np.concatenate([np.asarray(L0_ffn_sg_w), np.asarray(L0_ffn_su_w)], 0)), sd=rows(L0_ffn_sd_w),
        wexp=wexp, const=const)
    arrays = {k: np.ascontiguousarray(v) for k, v in arrays.items()}

    nc = bacc.Bacc("TRN2", target_bir_lowering=False, num_devices=1)
    aps = [nc.dram_tensor(n, arrays[n].shape, mybir.dt.from_np(arrays[n].dtype), kind="ExternalInput").ap()
           for n in _ARGS]
    out = nc.dram_tensor("out", (TOKENS, D), F32, kind="ExternalOutput").ap()
    build(nc, *aps, out)
    r = run_bass_kernel_spmd(nc, [arrays], core_ids=[0])
    return np.asarray(r.results[0]["out"]).reshape(NB, P, D)
```

```python
import concourse.bass as bass
from concourse import mybir
from contextlib import ExitStack

F32 = mybir.dt.float32
BF16 = mybir.dt.bfloat16
I32 = mybir.dt.int32
ALU = mybir.AluOpType
ACT = mybir.ActivationFunctionType
AX = mybir.AxisListType.X
SP, PE = mybir.EngineType.SP, mybir.EngineType.PE

P = 128
NB = 16
NG = 4
D = 256
KT = D // P
TOKENS = NB * P
HID = 32
HEADS, HD = 16, 16
GH = 4
NGRP = HEADS // GH
E, INTER, TOPK = 64, 128, 6
EG, TOPG = 8, 4
EPS = 1e-5
BIG = 3.0e38
NEG = -1.0e30

REGION = TOKENS + P
SLOTS = E * REGION
ROW = D + 2 * TOPK + 1
W_AT, S_AT, ID_AT = D, D + TOPK, D + 2 * TOPK
NTILES = (TOKENS * TOPK - E) // P + E
U = 8
NT = -(-NTILES // U) * U
RING = 8
NACC = 4
WCOLS = KT * 2 * INTER + D

_at = 0
C_AT = {}
for _name, _n in (("ident", P), ("causal", P), ("before", P), ("head", 8), ("ebase", E), ("ids", NB),
                  ("pad", ROW), ("upto", E), ("tile", NT), ("part", 1)):
    C_AT[_name] = (_at, _n)
    _at += _n
C_COLS = _at


def wait(eng, sem, n):
    if not isinstance(n, int) or n > 0:
        eng.wait_ge(sem, n)


def build(nc, x, w1t, b1, w2t, b2, wqkv, bqk, bv, wo, bo, gate, gbias, sgu, sd, wexp, const, out):
    ds = bass.ds
    slots_dram = nc.dram_tensor("slot_rows", (SLOTS + P, ROW), F32, kind="Internal").ap()
    acc_dram = [nc.dram_tensor(f"acc{a}", (TOKENS + P, D), F32, kind="Internal").ap() for a in range(NACC)]

    with ExitStack() as ctx:
        def sb(name, shape, dt=F32):
            return ctx.enter_context(nc.sbuf_tensor(name, shape, dt))

        def psum(name):
            return ctx.enter_context(nc.psum_tensor(name, [P, 512], F32))

        def sem(name):
            return ctx.enter_context(nc.semaphore(name))

        const_sb = sb("const_sb", [P, C_COLS])

        def c(name, rows=P):
            at, n = C_AT[name]
            return const_sb[0:rows, at:at + n]

        ident = c("ident")
        ident_b = sb("ident_b", [P, P], BF16)
        causal_b = sb("causal_b", [P, GH, P], BF16)
        before_b = sb("before_b", [P, P], BF16)
        ones_b = sb("ones_b", [P, P], BF16)
        upto_b = sb("upto_b", [E, E], BF16)
        ones_f = sb("ones_f", [P, P])
        w1_sb = sb("w1_sb", [P, HID])
        b1_sb = sb("b1_sb", [HID, 1])
        w2_sb = sb("w2_sb", [HID, NG, P])
        b2_sb = sb("b2_sb", [P, NG])
        wqkv_sb = sb("wqkv_sb", [P, KT, 3 * D])
        bqk_sb = sb("bqk_sb", [P, 4])
        bv_sb = sb("bv_sb", [P, D])
        wo_sb = sb("wo_sb", [P, KT, D])
        bo_sb = sb("bo_sb", [P, D])
        gate_sb = sb("gate_sb", [P, KT, E])
        gbias_sb = sb("gbias_sb", [P, E])
        gbias_half = sb("gbias_half", [P, E])
        sgu_sb = sb("sgu_sb", [P, KT, 2 * D])
        sd_sb = sb("sd_sb", [P, KT, D])

        x_sb = sb("x_sb", [P, NB, NG, D])
        xsum = sb("xsum", [P, NB])
        gel = sb("gel", [HID, 5, NB])
        wtok = sb("wtok", [P, NB, NG])
        wsm = sb("wsm", [P, 3, NB])
        wexpd = sb("wexpd", [P, NB, NG])
        wshift = sb("wshift", [P, NB, NG])
        h_all = sb("h_all", [P, NB, D])
        st = sb("st", [P, 2, 6])
        mv = sb("mv", [P, 2, 2])
        rs = sb("rs", [P, 4, 2])
        xn = sb("xn", [P, 2, D])
        xnt = sb("xnt", [P, 2, KT, P])
        qt = sb("qt", [P, 2, 2, P])
        kt = sb("kt", [P, 2, 2, P])
        kmask = sb("kmask", [P, 2, HEADS, P])
        vaug = sb("vaug", [P, 2, HEADS, 2 * HD])
        smax = sb("smax", [P, 2, GH])
        nmax = sb("nmax", [P, 2, GH])
        prob = sb("prob", [P, 2, GH, P])
        probt = sb("probt", [P, 2, GH, P])
        ot_sb = sb("ot_sb", [P, NGRP, P])
        rden = sb("rden", [P, HEADS])
        o_sb = sb("o_sb", [P, D])
        ont = sb("ont", [P, KT, P])
        row = sb("row", [P, 2, ROW])
        x2t = sb("x2t", [P, KT, P])
        gth = sb("gth", [P, E])
        score = sb("score", [P, E])
        gmx = sb("gmx", [P, EG + TOPG])
        gmx8 = sb("gmx8", [P, 8])
        gmr = sb("gmr", [P, EG + TOPG])
        gsel = sb("gsel", [P, EG])
        masked = sb("masked", [P, 2, E + 2])
        top8 = sb("top8", [P, 8])
        topr = sb("topr", [P, E + 2])
        tsum = sb("tsum", [P, 1])
        tinv = sb("tinv", [P, 2])
        sel_b = sb("sel_b", [P, 2, E], BF16)
        selsum = sb("selsum", [P, E], BF16)
        key0 = sb("key0", [P, E])
        key = sb("key", [P, E])
        key8 = sb("key8", [P, 8])
        wraw = sb("wraw", [P, TOPK])
        wjunk = sb("wjunk", [P, TOPK, E])
        slot_ix = sb("slot_ix", [P, 2, TOPK], I32)
        late = x_sb[:, :, 2:4, :].rearrange("p b g d -> p b (g d)")
        sth, sht = late[:, 0:2, :], late[:, 2:6, :].rearrange("p (t m) n -> p t m n", t=2)
        cnt_i = sb("cnt_i", [E, 2], I32)
        nt_f = sb("nt_f", [E, 3])
        nt_b = sb("nt_b", [E, 1], BF16)
        cum = sb("cum", [E, 1])
        past = sb("past", [E, NT])
        pad_ix = sb("pad_ix", [1, E], I32)
        tab = sb("tab", [1, 4, NT])
        tabf = sb("tabf", [1, 4, NT + 1])
        tab_i = sb("tab_i", [1, NT, 4], I32)
        rank_i = sb("rank_i", [1, NT], I32)
        myslot = sb("myslot", [P, NT])
        wring = sb("wring", [P, RING, WCOLS])
        free = kmask[:].rearrange("p t h k -> p (t h k)")
        xring = free[:, 0:U * ROW].rearrange("p (r n) -> p r n", n=ROW)
        y = free[:, U * ROW:U * ROW + NACC * D].rearrange("p (a n) -> p a n", n=D)
        spare = wring[:].rearrange("p r n -> p (r n)")
        junk, zeros = spare[:, 0:NG * D], spare[:, NG * D:NG * D + 1024]
        flat = x_sb[:].rearrange("p b g d -> p (b g d)")
        xt = prob[:, :, 0:KT, :]
        silu, hm, ht = probt[:, :, 0, :], probt[:, :, 1, :], probt[:, :, 2, :]
        wtile = sb("wtile", [P, NACC, 1])
        wtj = sb("wtj", [P, NACC, TOPK])

        ps = [psum(f"ps{i}") for i in range(8)]
        psS, psT, psO, psA, psX, psC = ps[0:2], ps[2:4], ps[4], ps[5], ps[6], ps[7]
        psG, psU, psD = ps[0:2], ps[2:4], ps[4:6]

        s = {}

        def S(name):
            if name not in s:
                s[name] = sem(name)
            return s[name]

        weights_in = [S(f"weights_in{i}") for i in range(15)]
        const_in = S("const_in")
        x_in = [S(f"x_in{i}") for i in range(4)]
        for name in ("consts_ready", "zeros_ready", "sum_act", "sum_dve", "tok_chain", "tok_hid", "tok_tanh", "tok_h",
                     "tok_w", "tok_shift", "tok_exp", "tok_ready",
                     "mix_chain", "ln1_done", "xn_transposed", "xnt_ready", "qk_done",
                     "q_ready", "k_ready", "kmask_ready", "v_done", "v_ready",
                     "scores_done", "max_done", "nmax_ready", "exp_done", "prob_transposed", "probt_ready",
                     "pv_done", "ot_ready", "ot_turned", "c2_chain", "o_ready", "o_transposed", "ont_ready",
                     "bias_added", "proj_done", "ln_chain", "x2_ready", "x2_transposed", "x2t_ready",
                     "gate_done", "gate_tanh", "g_chain", "score_read", "sel_ready", "pos_done", "key_read", "d_chain",
                     "pool_step", "gu_done", "gu_tanh", "sh_chain", "sh_mul", "shared_done", "h2_ready",
                     "row_ready",
                     "t_chain", "t_count", "t_cum", "t_past", "t_rows", "t_rowf", "t_bcast", "tab_ready",
                     "pad_ready", "myslot_ready",
                     "xt_done", "xt_ready", "up_done", "silu_done", "h_ready", "h_turned", "ht_ready",
                     "down_done", "wt_done", "y_ready", "fin_chain", "fin_ready"):
            S(name)
        scattered = [S(f"scattered{i}") for i in range(2)]
        acc_zero = S("acc_zero")
        padded = S("padded")
        w_in = [S(f"w_in{q}") for q in range(U)]
        xt_in = [S(f"xt_in{q}") for q in range(U)]
        added = [S(f"added{a}") for a in range(NACC)]
        fin_in = [S(f"fin_in{i}") for i in range(2)]
        fin_out = [S(f"fin_out{i}") for i in range(2)]

        CH = 4 * D
        NCH = TOKENS * D // P // CH
        fin_sb = flat.rearrange("p (i a n) -> p i a n", a=NACC, n=CH)

        block = ctx.enter_context(nc.Block())

        def image_loop(eng, step, first, last):
            for b in range(first, 4):
                step(b, b % 2)
            with eng.Fori(2, 6) as i:
                for par in range(2):
                    step(2 * i + par, par)
            for b in range(12, last + 1):
                step(b, b % 2)

        def has(b, lo=0, hi=NB - 1):
            return not isinstance(b, int) or lo <= b <= hi

        def tile_loop(eng, step, first, last):
            for t in range(first, U):
                step(0, t, t)
            with eng.Fori(1, NT // U - 1) as i:
                for q in range(U):
                    step(i, q, U * i + q)
            for t in range(NT - U, last + 1):
                step(NT // U - 1, t - (NT - U), t)

        def loaded(src, engine, most):
            why = "the table's making bounds it for any counts"
            _, vals = nc.values_load_multi_w_load_instructions(src, engines=[engine], min_val=0, max_val=max(most),
                                                               skip_runtime_bounds_check_because=why)
            return [nc.s_assert_within(v, 0, m, skip_runtime_bounds_check_because=why)
                    for v, m in zip(vals, most)]

        @block.sync
        def _(sp):
            sp.dma_start(const_sb[:], const).then_inc(const_in, 16)
            sp.dma_start(w1_sb[:], w1t).then_inc(weights_in[0], 16)
            sp.dma_start(b1_sb[:], b1).then_inc(weights_in[1], 16)
            for j in range(4):
                sp.dma_start(x_sb[:, 4 * j:4 * j + 4, :, :].rearrange("p b g d -> p (b g) d"),
                             x[4 * j:4 * j + 4].rearrange("b g c d -> c (b g) d")).then_inc(x_in[j], 16)
            sp.dma_start(w2_sb[:], w2t).then_inc(weights_in[2], 16)
            sp.dma_start(b2_sb[:], b2).then_inc(weights_in[3], 16)
            sp.dma_start(wqkv_sb[:], wqkv).then_inc(weights_in[4], 16)
            sp.dma_start(bqk_sb[:], bqk).then_inc(weights_in[5], 16)
            sp.dma_start(bv_sb[:], bv.to_broadcast([P, D])).then_inc(weights_in[6], 16)
            sp.dma_start(wo_sb[:], wo).then_inc(weights_in[7], 16)
            sp.dma_start(bo_sb[:], bo.to_broadcast([P, D])).then_inc(weights_in[8], 16)
            sp.dma_start(gbias_sb[:], gbias.to_broadcast([P, E])).then_inc(weights_in[9], 16)
            sp.dma_start(gate_sb[:], gate).then_inc(weights_in[10], 16)
            sp.dma_start(sgu_sb[:], sgu).then_inc(weights_in[11], 16)
            sp.dma_start(sd_sb[:], sd).then_inc(weights_in[12], 16)
            sp.wait_ge(const_in, 16)
            sp.wait_ge(S("zeros_ready"), 1)
            for a in range(NACC):
                for j in range(4):
                    sp.dma_start(acc_dram[a][j * 512:(j + 1) * 512, :].rearrange("(p n) d -> p (n d)", p=P),
                                 zeros).then_inc(acc_zero, 16)
                sp.dma_start(acc_dram[a][TOKENS:TOKENS + P, :], zeros[:, 0:D]).then_inc(acc_zero, 16)
            sp.dma_start(slots_dram[SLOTS:SLOTS + P, :], c("pad")).then_inc(acc_zero, 16)

            sp.wait_ge(S("pad_ready"), 1)
            with sp.Fori(0, E // 4) as e:
                for at in loaded(pad_ix[0:1, ds(4 * e, 4)], SP, (SLOTS - P,) * 4):
                    sp.dma_start(slots_dram[ds(at, P), :], c("pad")).then_inc(padded, 16)
            sp.wait_ge(padded, 16 * E)
            sp.wait_ge(acc_zero, 16 * (NACC * 5 + 1))
            for par in range(2):
                sp.wait_ge(scattered[par], 16 * TOPK * NB // 2)
            sp.wait_ge(S("tab_ready"), 4)

            def load_tile(i, q, t):
                wait(sp, S("down_done"), t - RING + 1)
                at, slot, ex, fresh = loaded(tab_i[0:1, ds(t, 1), :].rearrange("p a b -> p (a b)"), SP,
                                             (SLOTS, RING - 1, E - 1, 1))
                sp.dma_start(wring[:, ds(slot, 1), :], wexp[ds(ex, 1)].rearrange("a p d -> p a d"),
                             cond=fresh).then_inc(w_in[q], 16)
                wait(sp, added[q % NACC], 16 * ((U * i + q - q % NACC) // NACC - 1) if isinstance(i, int)
                     else 16 * (2 * i + q // NACC - 1))
                sp.dma_start(xring[:, q, :], slots_dram[ds(at, P), :]).then_inc(xt_in[q], 16)
            tile_loop(sp, load_tile, 0, NT - 1)

            def store(j):
                sp.wait_ge(S("fin_ready"), j + 1)
                sp.dma_start(out[j * 4 * P:(j + 1) * 4 * P, :].rearrange("(n p) d -> p n d", p=P),
                             fin_sb[:, j, 0, :].rearrange("p (n d) -> p n d", d=D)).then_inc(fin_out[j % 2], 16)

            for a in range(NACC):
                sp.wait_ge(added[a], 16 * (NT // NACC))
            for j in range(NCH):
                for a in range(NACC):
                    sp.dma_start(fin_sb[:, j, a, :].rearrange("p (n d) -> p n d", d=D),
                                 acc_dram[a][j * 4 * P:(j + 1) * 4 * P, :].rearrange(
                                     "(n p) d -> p n d", p=P)).then_inc(fin_in[j % 2], 16)
                if j:
                    store(j - 1)
            store(NCH - 1)
            for k in range(2):
                sp.wait_ge(fin_out[k], 16 * NCH // 2)

        @block.gpsimd
        def _(pool):
            nc.gpsimd.memset(zeros, 0.0).then_inc(S("zeros_ready"), 1)
            pool.wait_ge(const_in, 16)

            pool.wait_ge(weights_in[8], 16)

            def step(b, par):
                v, a, d = b + 1, b + 2, b - 3
                if has(v):
                    pool.wait_ge(S("ln1_done"), v + 1)
                    hb = h_all[:, ds(v, 1), :].rearrange("p a d -> p (a d)")
                    nc.gpsimd.tensor_tensor(hb, hb, bo_sb[:], ALU.add).then_inc(S("bias_added"), 1)
                if has(d):
                    pool.wait_ge(S("row_ready"), d + 1)
                    pool.sem_inc(S("pool_step"), 1)
                    for k in range(TOPK):
                        nc.gpsimd.indirect_dma_start(
                            out=slots_dram,
                            out_offset=bass.IndirectOffsetOnAxis(ap=slot_ix[:, 1 - par, k:k + 1], axis=0),
                            in_=row[:, 1 - par, :], in_offset=None).then_inc(scattered[1 - par], 16)
                if has(a):
                    pool.wait_ge(S("k_ready"), 2 * a + 2)
                    wait(pool, S("scores_done"), NGRP * (a - 1))
                    for m in range(2):
                        nc.gpsimd.tensor_tensor(
                            kmask[:, par, 8 * m:8 * m + 8, :],
                            kt[:, par, m, :].unsqueeze(1).to_broadcast([P, 8, P]),
                            c("head").unsqueeze(2).to_broadcast([P, 8, P]), ALU.mult).then_inc(S("kmask_ready"), 1)
            image_loop(pool, step, -2, NB + 2)

            def add_tile(i, q, t):
                a = q % NACC
                turn = 2 * i + q // NACC
                pool.wait_ge(S("y_ready"), t + 1)
                wait(pool, added[a], 16 * turn)
                pool.sem_inc(S("pool_step"), 1)
                nc.gpsimd.indirect_dma_start(
                    out=acc_dram[a],
                    out_offset=bass.IndirectOffsetOnAxis(ap=xring[:, q, ID_AT:ID_AT + 1].bitcast(I32), axis=0),
                    in_=y[:, a, :], in_offset=None, compute_op=ALU.add).then_inc(added[a], 16)
            tile_loop(pool, add_tile, 0, NT - 1)

        @block.scalar
        def _(act):
            for j in range(4):
                act.wait_ge(x_in[j], 16)
                for b in range(4 * j, 4 * j + 4, 2):
                    if b:
                        act.wait_ge(S("sum_act"), b // 2)
                    nc.scalar.activation(junk, x_sb[:, b, :, :].rearrange("p g d -> p (g d)"), ACT.Identity,
                                         accum_out=xsum[:, b:b + 1]).then_inc(S("sum_act"), 1)
            act.wait_ge(S("tok_hid"), 1)
            nc.scalar.activation(gel[:, 3, :], gel[:, 2, :], ACT.Tanh, scale=0.7978845608028654).then_inc(
                S("tok_tanh"), 1)
            act.wait_ge(S("tok_shift"), 1)
            nc.scalar.activation(wexpd[:], wshift[:], ACT.Exp).then_inc(S("tok_exp"), 1)

            act.wait_ge(weights_in[5], 16)

            def step(b, par):
                a, cc, d, q = b + 2, b - 1, b - 2, 1 - par

                def exp(img, g):
                    n, sp = NGRP * img + g, g % 2
                    act.wait_ge(S("nmax_ready"), n + 1)
                    wait(act, S("prob_transposed"), n - 1)
                    for j in range(GH):
                        last = nc.scalar.activation(prob[:, sp, j, :], psS[sp][:, j * P:(j + 1) * P], ACT.Exp,
                                                    bias=nmax[:, sp, j:j + 1], scale=HD ** -0.5)
                    last.then_inc(S("exp_done"), 1)

                def turn(g):
                    n, sp = NGRP * b + g, g % 2
                    act.wait_ge(S("prob_transposed"), n + 1)
                    wait(act, S("pv_done"), n - 1)
                    nc.scalar.copy(probt[:, sp].rearrange("p a k -> p (a k)"), psT[sp][:]).then_inc(
                        S("probt_ready"), 1)

                def project(m, dst, ready):
                    nc.scalar.activation(dst[:, par, m % 2, :], psA[:, m * P:(m + 1) * P], ACT.Identity,
                                         bias=bqk_sb[:, m:m + 1]).then_inc(S(ready), 1)

                if has(b):
                    turn(0)
                    exp(b, 1)
                    turn(1)
                if has(d):
                    act.wait_ge(S("x2_transposed"), d + 1)
                    wait(act, S("gate_done"), d)
                    nc.scalar.copy(x2t[:].rearrange("p a k -> p (a k)"), psX[:, 0:D]).then_inc(S("x2t_ready"), 1)
                if has(cc):
                    act.wait_ge(S("o_transposed"), cc + 1)
                    wait(act, S("proj_done"), cc)
                    nc.scalar.copy(ont[:].rearrange("p a k -> p (a k)"), psC[:, 0:D]).then_inc(S("ont_ready"), 1)
                if has(d):
                    nc.scalar.copy(x_sb[:, ds(d, 1), 1, :].rearrange("p a d -> p (a d)"), psX[:, 0:D]).then_inc(
                        S("x2t_ready"), 1)
                if has(b):
                    exp(b, 2)
                if has(a):
                    act.wait_ge(S("xn_transposed"), a + 1)
                    wait(act, S("v_done"), a - 1)
                    nc.scalar.copy(xnt[:, par].rearrange("p a k -> p (a k)"), psA[:, 0:D]).then_inc(
                        S("xnt_ready"), 1)
                if has(b):
                    turn(2)
                if has(d):
                    act.wait_ge(S("gate_done"), d + 1)
                    wait(act, S("score_read"), d)
                    nc.scalar.activation(gth[:], psX[:, 0:E], ACT.Tanh, scale=0.5).then_inc(S("gate_tanh"), 1)
                if has(b):
                    exp(b, 3)
                if has(a):
                    act.wait_ge(S("qk_done"), 2 * a + 1)
                    wait(act, S("kmask_ready"), 2 * (a - 1))
                    for m in (2, 3):
                        project(m, kt, "k_ready")
                if has(b):
                    turn(3)
                if has(b + 1):
                    exp(b + 1, 0)
                if has(b):
                    act.wait_ge(S("pv_done"), NGRP * (b + 1))
                    wait(act, S("ot_turned"), b)
                    nc.scalar.copy(ot_sb[:].rearrange("p a k -> p (a k)"), psO[:]).then_inc(S("ot_ready"), 1)
                if has(a):
                    act.wait_ge(S("qk_done"), 2 * a + 2)
                    wait(act, S("scores_done"), NGRP * (a - 1))
                    for m in (0, 1):
                        project(m, qt, "q_ready")
            image_loop(act, step, -2, NB + 1)

            for j in range(4):
                for m in range(2):
                    act.wait_ge(S("gu_done"), 4 * j + m + 1)
                    wait(act, S("sh_chain"), 2 * (j - 1) + m + 1)
                    nc.scalar.activation(sth[:, m, :], psG[m][:], ACT.Tanh, scale=0.5).then_inc(S("gu_tanh"), 1)

            def tile_step(i, q, t):
                u = t + 1
                if has(u, 0, NT - 1):
                    act.wait_ge(S("xt_done"), u + 1)
                    wait(act, S("up_done"), u - 1)
                    nc.scalar.copy(xt[:, (q + 1) % 2].rearrange("p a k -> p (a k)"),
                                   psT[(q + 1) % 2][:, 0:D]).then_inc(S("xt_ready"), 1)
                if has(t, 0, NT - 1):
                    act.wait_ge(S("up_done"), t + 1)
                    wait(act, S("h_ready"), t - 1)
                    nc.scalar.activation(silu[:, q % 2, :], psS[q % 2][:, 0:INTER], ACT.Silu).then_inc(
                        S("silu_done"), 1)
                if has(t - 1, 0, NT - 1):
                    act.wait_ge(S("h_turned"), t)
                    wait(act, S("down_done"), t - 2)
                    nc.scalar.copy(ht[:, (q + 1) % 2, :], ps[4 + (q + 1) % 2][:, 0:P]).then_inc(S("ht_ready"), 1)
            tile_loop(act, tile_step, -1, NT)

        @block.vector
        def _(dve):
            tok = [0]

            def link(ins, chain, base, count):
                count[0] += 1
                ins.then_inc(S(chain), 1)
                dve.wait_ge(S(chain), base + count[0])

            def start(chain):
                dve.sem_clear(S(chain))
                return [0]

            dve.wait_ge(const_in, 16)
            nc.vector.tensor_copy(ident_b[:], ident)
            for g in range(GH):
                nc.vector.tensor_copy(causal_b[:, g, :], c("causal"))
            nc.vector.tensor_copy(before_b[:], c("before"))
            nc.vector.tensor_copy(upto_b[:], c("upto", E))
            nc.vector.memset(ones_b[:], 1.0)
            nc.vector.memset(ones_f[:], 1.0)
            nc.vector.memset(selsum[:], 0.0)
            nc.vector.memset(gmx[:, EG:], BIG)
            nc.vector.memset(masked[:, :, E:], BIG)
            nc.vector.memset(vaug[:, :, :, HD + 1:], 0.0)
            nc.vector.memset(nt_f[:, 0:1], 1.0)
            nc.vector.memset(tabf[:, 2, 0:1], -1.0)
            nc.vector.memset(vaug[:, :, :, HD:HD + 1], 1.0).then_inc(S("consts_ready"), 1)
            dve.wait_ge(weights_in[9], 16)
            link(nc.vector.tensor_scalar(gbias_half[:], gbias_sb[:], 0.5, None, ALU.add), "tok_chain", 0, tok)

            for j in range(4):
                dve.wait_ge(x_in[j], 16)
                for b in range(4 * j + 1, 4 * j + 4, 2):
                    nc.vector.reduce_sum(xsum[:, b:b + 1], x_sb[:, b, :, :].rearrange("p g d -> p (g d)"),
                                         axis=AX).then_inc(S("sum_dve"), 1)
            dve.wait_ge(weights_in[1], 16)
            dve.wait_ge(S("tok_h"), 1)
            link(nc.vector.tensor_scalar(gel[:, 0, :], psA[0:HID, 0:NB], 1.0 / D, b1_sb[:, 0:1], ALU.mult, ALU.add),
                 "tok_chain", 0, tok)
            link(nc.vector.tensor_tensor(gel[:, 1, :], gel[:, 0, :], gel[:, 0, :], ALU.mult), "tok_chain", 0, tok)
            link(nc.vector.tensor_scalar(gel[:, 1, :], gel[:, 1, :], 0.044715, 1.0, ALU.mult, ALU.add),
                 "tok_chain", 0, tok)
            nc.vector.tensor_tensor(gel[:, 2, :], gel[:, 0, :], gel[:, 1, :], ALU.mult).then_inc(S("tok_hid"), 1)
            dve.wait_ge(S("tok_tanh"), 1)
            nc.vector.scalar_tensor_tensor(out=gel[:, 4, :], in0=gel[:, 3, :], scalar=1.0, in1=gel[:, 0, :],
                                           op0=ALU.add, op1=ALU.mult).then_inc(S("tok_hid"), 1)
            dve.wait_ge(S("tok_w"), 1)
            dve.wait_ge(weights_in[3], 16)
            link(nc.vector.scalar_tensor_tensor(
                out=wtok[:], in0=psA[:, 0:NG * NB].rearrange("p (g b) -> p b g", g=NG), scalar=0.5,
                in1=b2_sb[:].unsqueeze(1).to_broadcast([P, NB, NG]), op0=ALU.mult, op1=ALU.add),
                "tok_chain", 0, tok)
            link(nc.vector.tensor_reduce(wsm[:, 0, :], wtok[:], axis=AX, op=ALU.max), "tok_chain", 0, tok)
            nc.vector.tensor_tensor(wshift[:], wtok[:], wsm[:, 0, :].unsqueeze(2).to_broadcast([P, NB, NG]),
                                    ALU.subtract).then_inc(S("tok_shift"), 1)
            dve.wait_ge(S("tok_exp"), 1)
            link(nc.vector.tensor_reduce(wsm[:, 1, :], wexpd[:], axis=AX, op=ALU.add), "tok_chain", 0, tok)
            link(nc.vector.reciprocal(wsm[:, 2, :], wsm[:, 1, :]), "tok_chain", 0, tok)
            link(nc.vector.tensor_tensor(wtok[:], wexpd[:], wsm[:, 2, :].unsqueeze(2).to_broadcast([P, NB, NG]),
                                         ALU.mult), "tok_chain", 0, tok)

            def image(t, img):
                return t[:, ds(img, 1), :].rearrange("p a d -> p (a d)")

            def mix(a, g):
                hb = image(h_all, a)
                xg = x_sb[:, ds(a, 1), g, :].rearrange("p a d -> p (a d)")
                wg = wtok[:, ds(a, 1), g:g + 1].rearrange("p a d -> p (a d)")
                if g == 0:
                    dve.sem_clear(S("mix_chain"))
                    nc.vector.tensor_scalar(hb, xg, wg, None, ALU.mult).then_inc(S("mix_chain"), 1)
                    return
                dve.wait_ge(S("mix_chain"), g)
                nc.vector.scalar_tensor_tensor(out=hb, in0=xg, scalar=wg, in1=hb, op0=ALU.mult,
                                               op1=ALU.add).then_inc(S("mix_chain"), 1)

            ROOT = 11

            def root(k, lo, hi, base):
                v, y, r, z = (rs[:, n, lo:hi] for n in range(4))
                dve.wait_ge(S("ln_chain"), base + k)

                def done(ins):
                    ins.then_inc(S("ln_chain"), 1)
                if k == 0:
                    done(nc.vector.tensor_scalar(v, mv[:, lo:hi, 1], EPS, None, ALU.add))
                elif k == 1:
                    done(nc.vector.tensor_single_scalar(z.bitcast(I32), v.bitcast(I32), 1, ALU.arith_shift_right))
                elif k == 2:
                    done(nc.vector.tensor_scalar(y.bitcast(I32), z.bitcast(I32), -1.0, float(0x5F3759DF), ALU.mult,
                                                 ALU.add))
                elif k in (3, 8):
                    done(nc.vector.tensor_tensor(r, y, y, ALU.mult))
                elif k in (4, 9):
                    done(nc.vector.tensor_tensor(r, r, v, ALU.mult))
                elif k == 5:
                    done(nc.vector.tensor_scalar(z, r, 0.375, -1.25, ALU.mult, ALU.add))
                elif k == 6:
                    done(nc.vector.tensor_tensor(z, z, r, ALU.mult))
                elif k == 7:
                    done(nc.vector.scalar_tensor_tensor(out=y, in0=z, scalar=1.875, in1=y, op0=ALU.add,
                                                        op1=ALU.mult))
                elif k == 10:
                    done(nc.vector.tensor_scalar(z, r, -0.5, 1.5, ALU.mult, ALU.add))
                elif k == ROOT:
                    done(nc.vector.tensor_tensor(y, y, z, ALU.mult))

            def apply(src, dst, which):
                return nc.vector.tensor_scalar(dst, src, mv[:, which, 0:1], rs[:, 1, which:which + 1],
                                               ALU.subtract, ALU.mult)

            def smax_of(b, g):
                n, sp = NGRP * b + g, g % 2
                dve.wait_ge(S("scores_done"), n + 1)
                nc.vector.tensor_reduce(smax[:, sp, :], psS[sp][:].rearrange("p (a k) -> p a k", a=GH), axis=AX,
                                        op=ALU.max).then_inc(S("max_done"), 1)

            def nmax_of(b, g):
                n, sp = NGRP * b + g, g % 2
                dve.wait_ge(S("max_done"), n + 1)
                wait(dve, S("exp_done"), n - 1)
                nc.vector.tensor_scalar(nmax[:, sp, :], smax[:, sp, :], -HD ** -0.5, None, ALU.mult).then_inc(
                    S("nmax_ready"), 1)

            def v_evac(a, q):
                dve.wait_ge(S("v_done"), a + 1)
                wait(dve, S("pv_done"), NGRP * (a - 1))
                nc.vector.tensor_tensor(vaug[:, q, :, 0:HD], psA[:, 0:D].rearrange("p (h d) -> p h d", d=HD),
                                        bv_sb[:].rearrange("p (h d) -> p h d", d=HD), ALU.add).then_inc(
                    S("v_ready"), 1)

            o3 = psX[:].rearrange("p (h d) -> p h d", d=2 * HD)

            def den_of(cc):
                dve.wait_ge(S("ot_turned"), cc + 1)
                nc.vector.reciprocal(rden[:], o3[:, :, HD:HD + 1].rearrange("p h o -> p (h o)")).then_inc(
                    S("c2_chain"), 1)

            def normalise(cc):
                dve.wait_ge(S("c2_chain"), cc + 1)
                wait(dve, S("o_transposed"), cc)
                nc.vector.tensor_tensor(o_sb[:].rearrange("p (h d) -> p h d", d=HD), o3[:, :, 0:HD],
                                        rden[:].unsqueeze(2).to_broadcast([P, HEADS, HD]), ALU.mult).then_inc(
                    S("o_ready"), 1)

            ROUTE = 12

            def route(d, q, k):
                if k == 0:
                    dve.sem_clear(S("g_chain"))
                    dve.wait_ge(S("gate_tanh"), d + 1)
                    nc.vector.scalar_tensor_tensor(out=score[:], in0=gth[:], scalar=0.5, in1=gbias_half[:],
                                                   op0=ALU.mult, op1=ALU.add).then_inc(S("score_read"), 1)
                    return
                if k == 1:
                    dve.wait_ge(S("score_read"), d + 1)
                else:
                    dve.wait_ge(S("g_chain"), k - 1)
                mk = masked[:, q, :]

                def done(ins):
                    ins.then_inc(S("g_chain"), 1)
                if k == 1:
                    done(nc.vector.tensor_reduce(gmx[:, 0:EG], score[:].rearrange("p (g e) -> p g e", g=EG),
                                                 axis=AX, op=ALU.max))
                elif k == 2:
                    done(nc.vector.max(gmx8[:], gmx[:]))
                elif k == 3:
                    done(nc.vector.match_replace(gmr[:], gmx8[:], gmx[:], -BIG))
                elif k == 4:
                    done(nc.vector.tensor_scalar(gsel[:], gmr[:, 0:EG], -BIG, None, ALU.is_equal))
                elif k == 5:
                    done(nc.vector.tensor_tensor(mk[:, 0:E].rearrange("p (g e) -> p g e", g=EG),
                                                 score[:].rearrange("p (g e) -> p g e", g=EG),
                                                 gsel[:].unsqueeze(2).to_broadcast([P, EG, EG]), ALU.mult))
                elif k == 6:
                    done(nc.vector.max(top8[:], mk))
                elif k == 7:
                    done(nc.vector.match_replace(topr[:], top8[:], mk, -BIG))
                elif k == 8:
                    nc.vector.tensor_scalar(sel_b[:, q, :], topr[:, 0:E], -BIG, None, ALU.is_equal).then_inc(
                        S("sel_ready"), 1)
                    done(nc.vector.reduce_sum(tsum[:], top8[:, 2:8], axis=AX))
                elif k == 9:
                    done(nc.vector.tensor_scalar(tsum[:], tsum[:], 1e-8, None, ALU.add))
                elif k == 10:
                    done(nc.vector.reciprocal(tinv[:, q:q + 1], tsum[:]))
                elif k == 11:
                    done(nc.vector.tensor_copy(row[:, q, ID_AT:ID_AT + 1].bitcast(I32),
                                               c("ids")[:, ds(d, 1)].bitcast(I32)))
                elif k == ROUTE:
                    pass

            def place(d, q, k):
                if k == 0:
                    dve.sem_clear(S("d_chain"))
                    dve.wait_ge(S("pos_done"), d + 1)
                    nc.vector.tensor_tensor(key0[:], psC[:, 0:E], c("ebase"), ALU.add).then_inc(S("key_read"), 1)
                    nc.vector.tensor_tensor(selsum[:], selsum[:], sel_b[:, q, :], ALU.add).then_inc(
                        S("d_chain"), 1)
                elif k == 1:
                    dve.wait_ge(S("key_read"), d + 1)
                    nc.vector.tensor_tensor(key[:], key0[:], sel_b[:, q, :], ALU.mult).then_inc(S("d_chain"), 1)
                elif k == 2:
                    dve.wait_ge(S("d_chain"), 2)
                    nc.vector.max(key8[:], key[:]).then_inc(S("d_chain"), 1)
                elif k == 3:
                    dve.wait_ge(S("d_chain"), 3)
                    nc.vector.tensor_scalar(slot_ix[:, q, :], key8[:, 0:TOPK], 1.0, None, ALU.subtract)
                    nc.vector.tensor_scalar(row[:, q, S_AT:S_AT + TOPK], key8[:, 0:TOPK], 1.0, None, ALU.subtract)
                    for n in range(TOPK):
                        nc.vector.scalar_tensor_tensor(
                            out=wjunk[:, n, :], in0=key[:], scalar=key8[:, n:n + 1], in1=masked[:, q, 0:E],
                            op0=ALU.is_equal, op1=ALU.mult, accum_out=wraw[:, n:n + 1]).then_inc(S("d_chain"), 1)
                elif k == 4:
                    dve.wait_ge(S("d_chain"), 3 + TOPK)
                    nc.vector.tensor_scalar(row[:, q, W_AT:W_AT + TOPK], wraw[:], tinv[:, q:q + 1], None,
                                            ALU.mult).then_inc(S("row_ready"), 1)

            dve.wait_ge(weights_in[6], 16)

            def step(b, par):
                a, v, cc, d, e, q = b + 3, b + 1, b - 1, b - 2, b - 3, 1 - par
                if has(e):
                    place(e, q, 0)
                if has(cc):
                    den_of(cc)
                if has(e):
                    place(e, q, 1)
                if has(cc):
                    normalise(cc)
                if has(e):
                    place(e, q, 2)
                if has(b):
                    smax_of(b, 2)
                if has(e):
                    place(e, q, 3)
                if has(b):
                    nmax_of(b, 2)
                if has(e):
                    place(e, q, 4)
                if has(a):
                    mix(a, 0)
                if has(v):
                    v_evac(v, q)
                if has(a):
                    mix(a, 1)
                if has(b):
                    smax_of(b, 3)
                if has(a):
                    mix(a, 2)
                if has(b):
                    nmax_of(b, 3)
                if has(a):
                    mix(a, 3)

                lo, hi = 0 if has(a) else 1, 2 if has(cc) else 1
                ln = [0]

                def norm_step(ins):
                    ins.then_inc(S("ln_chain"), 1)
                    ln[0] += 1
                if hi > lo:
                    dve.sem_clear(S("ln_chain"))
                if has(d):
                    route(d, par, 0)
                if has(a):
                    dve.wait_ge(S("mix_chain"), NG)
                    norm_step(nc.vector.bn_stats(st[:, 0, :], image(h_all, a)))
                if has(d):
                    route(d, par, 1)
                if has(v):
                    smax_of(v, 0)
                if has(d):
                    route(d, par, 2)
                if has(v):
                    nmax_of(v, 0)
                if has(d):
                    route(d, par, 3)
                    route(d, par, 4)
                if has(cc):
                    dve.wait_ge(S("proj_done"), cc + 1)
                    dve.wait_ge(S("bias_added"), cc + 1)
                    norm_step(nc.vector.tensor_tensor(image(h_all, cc), image(h_all, cc), psC[:, D:2 * D], ALU.add))
                if has(d):
                    route(d, par, 5)
                if has(cc):
                    dve.wait_ge(S("ln_chain"), ln[0])
                    norm_step(nc.vector.bn_stats(st[:, 1, :], image(h_all, cc)))
                if has(d):
                    route(d, par, 6)
                at = ln[0]
                for w in range(lo, hi):
                    dve.wait_ge(S("ln_chain"), at)
                    norm_step(nc.vector.bn_aggr(mv[:, w, :], st[:, w, :]))
                at = ln[0]
                for k in range(ROOT + 1):
                    if has(d) and k + 7 <= ROUTE:
                        route(d, par, k + 7)
                    if hi > lo:
                        root(k, lo, hi, at)
                    if has(v) and k == 7:
                        smax_of(v, 1)
                    if has(v) and k == 9:
                        nmax_of(v, 1)
                if has(cc):
                    dve.wait_ge(S("ln_chain"), at + ROOT + 1)
                    wait(dve, scattered[q], 8 * TOPK * (cc - q))
                    apply(image(h_all, cc), row[:, q, 0:D], 1).then_inc(S("x2_ready"), 1)
                if has(a):
                    dve.wait_ge(S("ln_chain"), at + ROOT + 1)
                    wait(dve, S("xn_transposed"), a - 1)
                    apply(image(h_all, a), xn[:, q, :], 0).then_inc(S("ln1_done"), 1)
            image_loop(dve, step, -3, NB + 2)

            tn = [0]

            def lt(ins):
                link(ins, "t_chain", 0, tn)
            dve.wait_ge(S("t_count"), 1)
            lt(nc.vector.tensor_scalar(cnt_i[:, 0:1], psX[0:E, 0:1], float(P - 1), None, ALU.add))
            lt(nc.vector.tensor_single_scalar(cnt_i[:, 1:2], cnt_i[:, 0:1], 7, ALU.arith_shift_right))
            lt(nc.vector.tensor_copy(nt_f[:, 1:2], cnt_i[:, 1:2]))
            nc.vector.tensor_scalar(nt_f[:, 2:3], nt_f[:, 1:2], 0.0, None, ALU.is_gt)
            lt(nc.vector.scalar_tensor_tensor(out=tab[:, 0, 0:E], in0=psX[0:1, E:2 * E], scalar=-1.0,
                                              in1=c("ebase", 1), op0=ALU.add, op1=ALU.add))
            nc.vector.tensor_copy(pad_ix[:], tab[:, 0, 0:E]).then_inc(S("pad_ready"), 1)
            nc.vector.tensor_copy(nt_b[:], nt_f[:, 1:2]).then_inc(S("t_rows"), 1)
            dve.wait_ge(S("t_cum"), 1)
            lt(nc.vector.tensor_copy(cum[:], psX[0:E, 0:1]))
            nc.vector.tensor_scalar(past[:], c("tile", E), cum[:, 0:1], None, ALU.is_ge).then_inc(S("t_rows"), 1)
            dve.wait_ge(S("t_past"), 1)
            ex, before, rank = (psX[0:1, k * NT:(k + 1) * NT] for k in range(3))
            lt(nc.vector.tensor_tensor(tab[:, 1, :], c("tile", 1), before, ALU.subtract))
            lt(nc.vector.tensor_scalar(tab[:, 1, :], tab[:, 1, :], float(P), None, ALU.mult))
            lt(nc.vector.scalar_tensor_tensor(out=tab[:, 2, :], in0=ex, scalar=float(REGION), in1=tab[:, 1, :],
                                              op0=ALU.mult, op1=ALU.add))
            nc.vector.tensor_scalar(tab[:, 3, :], tab[:, 2, :], float(SLOTS), None, ALU.min).then_inc(
                S("t_rowf"), 1)
            dve.wait_ge(S("t_rowf"), 1)
            nc.vector.tensor_copy(tab_i[:, :, 0], tab[:, 3, :]).then_inc(S("tab_ready"), 1)
            nc.vector.tensor_scalar(tab_i[:, :, 2], ex, float(E - 1), None, ALU.min).then_inc(S("tab_ready"), 1)
            lt(nc.vector.tensor_copy(rank_i[:], rank))
            lt(nc.vector.tensor_copy(tabf[:, 2, 1:NT + 1], rank))
            nc.vector.tensor_single_scalar(tab_i[:, :, 1], rank_i[:], RING - 1, ALU.bitwise_and).then_inc(
                S("tab_ready"), 1)
            nc.vector.tensor_tensor(tab_i[:, :, 3], tabf[:, 2, 1:NT + 1], tabf[:, 2, 0:NT],
                                    ALU.not_equal).then_inc(S("tab_ready"), 1)
            dve.wait_ge(S("t_bcast"), 1)
            nc.vector.tensor_scalar(myslot[:], psC[:, 0:NT], c("part"), None, ALU.add).then_inc(
                S("myslot_ready"), 1)
            dve.wait_ge(S("myslot_ready"), 1)

            for j in range(4):
                for m in range(2):
                    dve.wait_ge(S("gu_tanh"), 2 * j + m + 1)
                    nc.vector.scalar_tensor_tensor(out=sth[:, m, :], in0=sth[:, m, :], scalar=1.0, in1=psG[m][:],
                                                   op0=ALU.add, op1=ALU.mult).then_inc(S("sh_mul"), 1)
                for m in range(2):
                    dve.wait_ge(S("gu_done"), 4 * j + 3 + m)
                    dve.wait_ge(S("sh_mul"), 2 * j + m + 1)
                    wait(dve, S("shared_done"), 4 * (j - 1))
                    nc.vector.scalar_tensor_tensor(out=sht[:, j % 2, m, :], in0=sth[:, m, :], scalar=0.5,
                                                   in1=psU[m][:], op0=ALU.mult, op1=ALU.mult).then_inc(
                        S("sh_chain"), 1)
                    if m:
                        dve.wait_ge(S("sh_chain"), 2 * j + 2)
                for n in range(4):
                    hb = h_all[:, 4 * j + n, :]
                    dve.wait_ge(S("shared_done"), 4 * j + n + 1)
                    nc.vector.tensor_tensor(hb, hb, psD[n % 2][:, 0:D], ALU.add).then_inc(S("h2_ready"), 1)

            def tile_step(i, q, t):
                if has(t, 0, NT - 1):
                    dve.wait_ge(xt_in[q], 16 * i + 16)
                    wait(dve, S("y_ready"), t - NACC + 1)
                    nc.vector.scalar_tensor_tensor(
                        out=wtj[:, q % NACC, :], in0=xring[:, q, S_AT:S_AT + TOPK], scalar=myslot[:, ds(t, 1)],
                        in1=xring[:, q, W_AT:W_AT + TOPK], op0=ALU.is_equal, op1=ALU.mult,
                        accum_out=wtile[:, q % NACC, :]).then_inc(S("wt_done"), 1)
                    dve.wait_ge(S("silu_done"), t + 1)
                    wait(dve, S("h_turned"), t - 1)
                    nc.vector.tensor_tensor(hm[:, q % 2, :], silu[:, q % 2, :], psS[q % 2][:, INTER:2 * INTER],
                                            ALU.mult).then_inc(S("h_ready"), 1)
                v, a = t - 2, (q - 2) % NACC
                if has(v, 0, NT - 1):
                    dve.wait_ge(S("down_done"), t - 1)
                    dve.wait_ge(S("wt_done"), t - 1)
                    turn = (2 * i + (q - 2) // NACC)
                    wait(dve, added[a], 16 * turn)
                    nc.vector.tensor_scalar(y[:, a, :], ps[6 + q % 2][:, 0:D], wtile[:, a, :], None,
                                            ALU.mult).then_inc(S("y_ready"), 1)
            tile_loop(dve, tile_step, 0, NT + 1)

            for j in range(NCH):
                base = 3 * j
                dve.wait_ge(fin_in[j % 2], 16 * NACC * (j // 2 + 1))
                f = [fin_sb[:, j, a, :] for a in range(NACC)]
                rest = h_all[:, 4 * j:4 * j + 4, :].rearrange("p b d -> p (b d)")
                dve.wait_ge(S("h2_ready"), 4 * j + 4)
                nc.vector.tensor_tensor(f[0], f[0], f[1], ALU.add).then_inc(S("fin_chain"), 1)
                nc.vector.tensor_tensor(f[2], f[2], f[3], ALU.add).then_inc(S("fin_chain"), 1)
                dve.wait_ge(S("fin_chain"), base + 1)
                nc.vector.tensor_tensor(f[0], f[0], rest, ALU.add).then_inc(S("fin_chain"), 1)
                dve.wait_ge(S("fin_chain"), base + 3)
                nc.vector.tensor_tensor(f[0], f[0], f[2], ALU.add).then_inc(S("fin_ready"), 1)

        @block.tensor
        def _(pe):
            def mm(*a, **k):
                return nc.tensor.matmul(*a, **k)

            def both(dst, lhs, rhs):
                for k in range(KT):
                    last = mm(dst, lhs(k), rhs(k), start=k == 0, stop=k == KT - 1)
                return last

            pe.wait_ge(weights_in[0], 16)
            pe.wait_ge(S("sum_act"), NB // 2)
            pe.wait_ge(S("sum_dve"), NB // 2)
            mm(psA[0:HID, 0:NB], w1_sb[:], xsum[:], start=True, stop=True).then_inc(S("tok_h"), 1)
            pe.wait_ge(weights_in[2], 16)
            pe.wait_ge(S("tok_hid"), 2)
            for g in range(NG):
                last = mm(psA[:, g * NB:(g + 1) * NB], w2_sb[:, g, :], gel[:, 4, :], start=True, stop=True)
            last.then_inc(S("tok_w"), 1)
            for k in (4, 7, 10, 11, 12):
                pe.wait_ge(weights_in[k], 16)
            pe.wait_ge(S("consts_ready"), 1)

            def step(b, par):
                a, v, cc, d, e, q = b + 2, b + 1, b - 1, b - 2, b - 3, 1 - par

                def scores(img, g, p):
                    n, sp = NGRP * img + g, g % 2
                    if g == 0:
                        pe.wait_ge(S("kmask_ready"), 2 * img + 2)
                        pe.wait_ge(S("q_ready"), 2 * img + 2)
                    wait(pe, S("exp_done"), n - 1)
                    mm(psS[sp][:], ident_b[:], causal_b[:].rearrange("p a k -> p (a k)"), start=True, stop=False)
                    mm(psS[sp][:], qt[:, p, g // 2, :],
                       kmask[:, p, GH * g:GH * g + GH, :].rearrange("p a k -> p (a k)"),
                       start=False, stop=True).then_inc(S("scores_done"), 1)

                def turn(g):
                    n, sp = NGRP * b + g, g % 2
                    pe.wait_ge(S("exp_done"), n + 1)
                    wait(pe, S("probt_ready"), n - 1)
                    for j in range(GH):
                        last = nc.tensor.transpose(psT[sp][:, j * P:(j + 1) * P], prob[:, sp, j, :], ident)
                    last.then_inc(S("prob_transposed"), 1)

                def pv(g):
                    n, sp = NGRP * b + g, g % 2
                    pe.wait_ge(S("probt_ready"), n + 1)
                    if g == 0:
                        pe.wait_ge(S("v_ready"), b + 1)
                        wait(pe, S("ot_ready"), b)
                    for j in range(GH):
                        last = mm(psO[32 * j:32 * j + 32, g * P:(g + 1) * P], vaug[:, par, GH * g + j, :],
                                  probt[:, sp, j, :], start=True, stop=True)
                    last.then_inc(S("pv_done"), 1)

                def two(dst, src, done):
                    for k in range(KT):
                        last = nc.tensor.transpose(dst[:, k * P:(k + 1) * P], src[:, k * P:(k + 1) * P], ident)
                    last.then_inc(S(done), 1)

                def project(which):
                    for m in which:
                        last = both(psA[:, m * P:(m + 1) * P], lambda k: wqkv_sb[:, k, m * P:(m + 1) * P],
                                    lambda k: xnt[:, par, k, :])
                    last.then_inc(S("qk_done"), 1)

                if has(e):
                    pe.wait_ge(S("sel_ready"), e + 1)
                    mm(psC[:, 0:E], before_b[:], sel_b[:, q, :], start=True, stop=False)
                    mm(psC[:, 0:E], ones_b[:], selsum[:], start=False, stop=True).then_inc(S("pos_done"), 1)
                if has(b):
                    turn(0)
                if has(cc):
                    pe.wait_ge(S("ot_ready"), cc + 1)
                    wait(pe, S("gate_tanh"), cc - 1)
                    for g in range(NGRP):
                        last = nc.tensor.transpose(psX[:, g * P:(g + 1) * P], ot_sb[:, g, :], ident)
                    last.then_inc(S("ot_turned"), 1)
                if has(b):
                    scores(b, 2, par)
                    pv(0)
                if has(v):
                    wait(pe, S("q_ready"), 2 * v + 2)
                    both(psA[:, 0:D], lambda k: xnt[:, q, k, :], lambda k: wqkv_sb[:, k, 2 * D:3 * D]).then_inc(
                        S("v_done"), 1)
                if has(d):
                    pe.wait_ge(S("x2_ready"), d + 1)
                    wait(pe, S("o_ready"), cc + 1 if not isinstance(cc, int) else min(cc + 1, NB))
                    two(psX, row[:, par, :], "x2_transposed")
                if has(b):
                    turn(1)
                    scores(b, 3, par)
                if has(cc):
                    pe.wait_ge(S("o_ready"), cc + 1)
                    wait(pe, S("key_read"), e + 1)
                    two(psC, o_sb, "o_transposed")
                if has(b):
                    pv(1)
                if has(a):
                    pe.wait_ge(S("ln1_done"), a + 1)
                    wait(pe, S("v_ready"), a)
                    two(psA, xn[:, par, :], "xn_transposed")
                if has(d):
                    pe.wait_ge(S("x2t_ready"), 2 * d + 2)
                    both(psX[:, 0:E], lambda k: x2t[:, k, :], lambda k: gate_sb[:, k, :]).then_inc(
                        S("gate_done"), 1)
                if has(b):
                    turn(2)
                if has(v):
                    scores(v, 0, q)
                if has(b):
                    pv(2)
                if has(cc):
                    pe.wait_ge(S("ont_ready"), cc + 1)
                    wait(pe, S("x2_ready"), cc)
                    both(psC[:, D:2 * D], lambda k: ont[:, k, :], lambda k: wo_sb[:, k, :]).then_inc(
                        S("proj_done"), 1)
                if has(a):
                    pe.wait_ge(S("xnt_ready"), a + 1)
                    project((2, 3))
                if has(b):
                    turn(3)
                if has(v):
                    scores(v, 1, q)
                if has(b):
                    pv(3)
                if has(a):
                    pe.wait_ge(S("k_ready"), 2 * a + 2)
                    project((0, 1))
            image_loop(pe, step, -2, NB + 2)

            def shared_up(j, m):
                if j:
                    if m < 2:
                        pe.wait_ge(S("sh_mul"), 2 * (j - 1) + m + 1)
                    else:
                        pe.wait_ge(S("sh_chain"), 2 * (j - 1) + m - 1)
                x4 = x_sb[:, 4 * j:4 * j + 4, 1, :]
                both((psG + psU)[m][:], lambda k: sgu_sb[:, k, m * P:(m + 1) * P],
                     lambda k: x4[:, :, k * P:(k + 1) * P]).then_inc(S("gu_done"), 1)

            def shared_down(j):
                pe.wait_ge(S("sh_chain"), 2 * j + 2)
                for n in range(4):
                    wait(pe, S("h2_ready"), 4 * j + n - 1)
                    both(psD[n % 2][:, 0:D], lambda k: sht[:, j % 2, k, n * P:(n + 1) * P],
                         lambda k: sd_sb[:, k, :]).then_inc(S("shared_done"), 1)

            pe.wait_ge(S("x2t_ready"), 2 * NB)
            pe.wait_ge(S("row_ready"), NB)
            mm(psX[0:E, 0:1], selsum[:], ones_b[:, 0:1], start=True, stop=True)
            mm(psX[0:1, E:2 * E], ones_b[:, 0:1], selsum[:], start=True, stop=True).then_inc(S("t_count"), 1)
            shared_up(0, 0)
            pe.wait_ge(S("t_rows"), 1)
            mm(psX[0:E, 0:1], upto_b[:], nt_b[:], start=True, stop=True).then_inc(S("t_cum"), 1)
            shared_up(0, 1)
            pe.wait_ge(S("t_rows"), 2)
            for k in range(3):
                last = mm(psX[0:1, k * NT:(k + 1) * NT], nt_f[:, k:k + 1], past[:], start=True, stop=True)
            last.then_inc(S("t_past"), 1)
            shared_up(0, 2)
            pe.wait_ge(S("t_rowf"), 1)
            mm(psC[:, 0:NT], ones_f[0:1, :], tab[:, 3, :], start=True, stop=True).then_inc(S("t_bcast"), 1)
            shared_up(0, 3)
            for j in range(4):
                if j < 3:
                    for m in range(2):
                        shared_up(j + 1, m)
                shared_down(j)
                if j < 3:
                    for m in range(2, 4):
                        shared_up(j + 1, m)
            pe.wait_ge(S("tab_ready"), 4)
            pe.wait_ge(S("myslot_ready"), 1)
            pe.wait_ge(S("h2_ready"), 16)

            def tile_step(i, q, t):
                u = t + 1
                if has(u, 0, NT - 1):
                    uq = (q + 1) % U
                    turn = i if q < U - 1 else i + 1
                    if isinstance(i, int) and t == -1:
                        turn = 0
                    pe.wait_ge(xt_in[uq], 16 * turn + 16)
                    wait(pe, S("xt_ready"), u - 1)
                    for k in range(KT):
                        last = nc.tensor.transpose(psT[uq % 2][:, k * P:(k + 1) * P],
                                                   xring[:, uq, k * P:(k + 1) * P], ident)
                    last.then_inc(S("xt_done"), 1)
                if has(t, 0, NT - 1):
                    slot, = loaded(tab_i[0:1, ds(t, 1), 1:2].rearrange("p a b -> p (a b)"), PE, (RING - 1,))
                    pe.wait_ge(S("xt_ready"), t + 1)
                    pe.wait_ge(w_in[q], 16 * i + 16)
                    wait(pe, S("h_ready"), t - 1)
                    both(psS[q % 2][:, 0:2 * INTER], lambda k: xt[:, q % 2, k, :],
                         lambda k: wring[:, ds(slot, 1), k * 2 * INTER:(k + 1) * 2 * INTER]).then_inc(
                        S("up_done"), 1)
                v = t - 1
                if has(v, 0, NT - 1):
                    vq = (q - 1) % 2
                    pe.wait_ge(S("h_ready"), v + 1)
                    wait(pe, S("ht_ready"), v - 1)
                    nc.tensor.transpose(ps[4 + vq][:, 0:P], hm[:, vq, :], ident).then_inc(S("h_turned"), 1)
                v = t - 2
                if has(v, 0, NT - 1):
                    vq = q % 2
                    slot, = loaded(tab_i[0:1, ds(v, 1), 1:2].rearrange("p a b -> p (a b)"), PE, (RING - 1,))
                    pe.wait_ge(S("ht_ready"), v + 1)
                    wait(pe, S("y_ready"), v - 1)
                    mm(ps[6 + vq][:, 0:D], ht[:, vq, :], wring[:, ds(slot, 1), KT * 2 * INTER:WCOLS],
                       start=True, stop=True).then_inc(S("down_done"), 1)
            tile_loop(pe, tile_step, -1, NT + 1)


_ARGS = ("x", "w1t", "b1", "w2t", "b2", "wqkv", "bqk", "bv", "wo", "bo", "gate", "gbias", "sgu", "sd", "wexp",
         "const")


def kernel(x, L0_tok_w1, L0_tok_b1, L0_tok_w2, L0_tok_b2, L0_attn_W_qkv, L0_attn_b_qkv, L0_attn_W_o, L0_attn_b_o,
           L0_ffn_gate_w, L0_ffn_gate_bias, L0_ffn_eg_w, L0_ffn_eu_w, L0_ffn_ed_w, L0_ffn_sg_w, L0_ffn_su_w,
           L0_ffn_sd_w):
    import numpy as np
    import concourse.bacc as bacc
    from concourse.bass_utils import run_bass_kernel_spmd

    def rows(w):
        w = np.asarray(w)
        return np.ascontiguousarray(w.T.reshape(KT, P, w.shape[0]).transpose(1, 0, 2))

    const = np.zeros((P, C_COLS), np.float32)

    def put(name, v):
        at, n = C_AT[name]
        const[:, at:at + n] = v
    p = np.arange(P)
    put("ident", np.eye(P))
    put("causal", np.where(p[None, :] > p[:, None], NEG, 0.0))
    put("before", p[:, None] < p[None, :])
    put("head", p[:, None] // HD == np.arange(8)[None, :])
    put("ebase", np.arange(E)[None, :] * REGION + 1)
    put("ids", (np.arange(NB)[None, :] * P + p[:, None]).astype(np.int32).view(np.float32))
    pad = np.zeros((P, ROW), np.float32)
    pad[:, S_AT:S_AT + TOPK] = -1.0
    pad[:, ID_AT] = (TOKENS + p).astype(np.int32).view(np.float32)
    put("pad", pad)
    put("upto", p[:, None] <= np.arange(E)[None, :])
    put("tile", np.arange(NT)[None, :])
    put("part", p[:, None])

    eg, eu, ed = (np.asarray(w) for w in (L0_ffn_eg_w, L0_ffn_eu_w, L0_ffn_ed_w))
    up = np.stack([eg, eu], 1).reshape(E, 2 * INTER, KT, P).transpose(0, 3, 2, 1).reshape(E, P, KT * 2 * INTER)
    wexp = np.ascontiguousarray(np.concatenate([up, ed.transpose(0, 2, 1)], 2))
    bqkv = np.asarray(L0_attn_b_qkv)
    arrays = dict(
        x=np.asarray(x), w1t=np.ascontiguousarray(np.asarray(L0_tok_w1).T), b1=np.asarray(L0_tok_b1)[:, None],
        w2t=np.ascontiguousarray(np.asarray(L0_tok_w2).reshape(P, NG, HID).transpose(2, 1, 0)),
        b2=np.asarray(L0_tok_b2).reshape(P, NG), wqkv=rows(L0_attn_W_qkv),
        bqk=np.ascontiguousarray(bqkv[:2 * D].reshape(4, P).T), bv=bqkv[2 * D:][None, :], wo=rows(L0_attn_W_o),
        bo=np.asarray(L0_attn_b_o)[None, :], gate=rows(L0_ffn_gate_w), gbias=np.asarray(L0_ffn_gate_bias)[None, :],
        sgu=rows(np.concatenate([np.asarray(L0_ffn_sg_w), np.asarray(L0_ffn_su_w)], 0)), sd=rows(L0_ffn_sd_w),
        wexp=wexp, const=const)
    arrays = {k: np.ascontiguousarray(v) for k, v in arrays.items()}

    nc = bacc.Bacc("TRN2", target_bir_lowering=False, num_devices=1)
    aps = [nc.dram_tensor(n, arrays[n].shape, mybir.dt.from_np(arrays[n].dtype), kind="ExternalInput").ap()
           for n in _ARGS]
    out = nc.dram_tensor("out", (TOKENS, D), F32, kind="ExternalOutput").ap()
    build(nc, *aps, out)
    r = run_bass_kernel_spmd(nc, [arrays], core_ids=[0])
    return np.asarray(r.results[0]["out"]).reshape(NB, P, D)
```

```python
import concourse.bass as bass
from concourse import mybir
from contextlib import ExitStack

F32 = mybir.dt.float32
BF16 = mybir.dt.bfloat16
I32 = mybir.dt.int32
ALU = mybir.AluOpType
ACT = mybir.ActivationFunctionType
AX = mybir.AxisListType.X
SP, PE, POOL = mybir.EngineType.SP, mybir.EngineType.PE, mybir.EngineType.Pool
SCALAR, VECTOR = mybir.EngineType.Activation, mybir.EngineType.DVE

P = 128
NB = 16
NG = 4
D = 256
KT = D // P
TOKENS = NB * P
HID = 32
HEADS, HD = 16, 16
GH = 4
NGRP = HEADS // GH
E, INTER, TOPK = 64, 128, 6
EG, TOPG = 8, 4
EPS = 1e-5
BIG = 3.0e38
NEG = -1.0e30

REGION = TOKENS + P
SLOTS = E * REGION
ROW = D + 2 * TOPK + 1
W_AT, S_AT, ID_AT = D, D + TOPK, D + 2 * TOPK
NTILES = (TOKENS * TOPK - E) // P + E
U = 12
TURNS = -(-NTILES // U)
NT = TURNS * U
SLOTS_AT = -(-(U + 2) // 4) * 4
NTAB = NT + 2
RING = 8
NACC = 3
WCOLS = KT * 2 * INTER + D

_at = 0
C_AT = {}
for _name, _n in (("ident", P), ("causal", P), ("before", P), ("head", 8), ("ebase", E), ("ids", NB),
                  ("pad", ROW), ("upto", E), ("tile", NTAB), ("part", 1)):
    C_AT[_name] = (_at, _n)
    _at += _n
C_COLS = _at


def wait(eng, sem, n):
    if not isinstance(n, int) or n > 0:
        eng.wait_ge(sem, n)


def build(nc, x, w1t, b1, w2t, b2, wqkv, bqk, bv, wo, bo, gate, gbias, sgu, sd, wexp, const, out):
    ds = bass.ds
    slots_dram = nc.dram_tensor("slot_rows", (SLOTS + P, ROW), F32, kind="Internal").ap()
    acc_dram = [nc.dram_tensor(f"acc{a}", (TOKENS + P, D), F32, kind="Internal").ap() for a in range(NACC)]

    with ExitStack() as ctx:
        def sb(name, shape, dt=F32):
            return ctx.enter_context(nc.sbuf_tensor(name, shape, dt))

        def psum(name):
            return ctx.enter_context(nc.psum_tensor(name, [P, 512], F32))

        def sem(name):
            return ctx.enter_context(nc.semaphore(name))

        const_sb = sb("const_sb", [P, C_COLS])

        def c(name, rows=P):
            at, n = C_AT[name]
            return const_sb[0:rows, at:at + n]

        ident = c("ident")
        ident_b = sb("ident_b", [P, P], BF16)
        causal_b = sb("causal_b", [P, GH, P], BF16)
        before_b = sb("before_b", [P, P], BF16)
        ones_b = sb("ones_b", [P, P], BF16)
        upto_b = sb("upto_b", [E, E], BF16)
        ones_f = sb("ones_f", [P, P])
        w1_sb = sb("w1_sb", [P, HID])
        b1_sb = sb("b1_sb", [HID, 1])
        w2_sb = sb("w2_sb", [HID, NG, P])
        b2_sb = sb("b2_sb", [P, NG])
        wqkv_sb = sb("wqkv_sb", [P, KT, 3 * D])
        bqk_sb = sb("bqk_sb", [P, 4])
        bv_sb = sb("bv_sb", [P, D])
        wo_sb = sb("wo_sb", [P, KT, D])
        bo_sb = sb("bo_sb", [P, D])
        gate_sb = sb("gate_sb", [P, KT, E])
        gbias_sb = sb("gbias_sb", [P, E])
        gbias_half = sb("gbias_half", [P, E])
        sgu_sb = sb("sgu_sb", [P, KT, 2 * D])
        sd_sb = sb("sd_sb", [P, KT, D])

        x_sb = sb("x_sb", [P, NB, NG, D])
        xsum = sb("xsum", [P, NB])
        gel = sb("gel", [HID, 5, NB])
        wtok = sb("wtok", [P, NB, NG])
        wsm = sb("wsm", [P, 3, NB])
        wexpd = sb("wexpd", [P, NB, NG])
        wshift = sb("wshift", [P, NB, NG])
        h_all = sb("h_all", [P, NB, D])
        st = sb("st", [P, 2, 6])
        mv = sb("mv", [P, 2, 2])
        rs = sb("rs", [P, 4, 2])
        xn = sb("xn", [P, 2, D])
        xnt = sb("xnt", [P, 2, KT, P])
        qt = sb("qt", [P, 2, 2, P])
        kt = sb("kt", [P, 2, 2, P])
        kmask = sb("kmask", [P, 2, HEADS, P])
        vaug = sb("vaug", [P, 2, HEADS, 2 * HD])
        smax = sb("smax", [P, 2, GH])
        nmax = sb("nmax", [P, 2, GH])
        prob = sb("prob", [P, 2, GH, P])
        probt = sb("probt", [P, 2, GH, P])
        ot_sb = sb("ot_sb", [P, NGRP, P])
        rden = sb("rden", [P, HEADS])
        o_sb = sb("o_sb", [P, D])
        ont = sb("ont", [P, KT, P])
        row = sb("row", [P, 2, ROW])
        x2t = sb("x2t", [P, KT, P])
        gth = sb("gth", [P, E])
        score = sb("score", [P, E])
        gmx = sb("gmx", [P, EG + TOPG])
        gmx8 = sb("gmx8", [P, 8])
        gmr = sb("gmr", [P, EG + TOPG])
        gsel = sb("gsel", [P, EG])
        masked = sb("masked", [P, 2, E + 2])
        top8 = sb("top8", [P, 8])
        topr = sb("topr", [P, E + 2])
        tsum = sb("tsum", [P, 1])
        tinv = sb("tinv", [P, 2])
        sel_b = sb("sel_b", [P, 2, E], BF16)
        selsum = sb("selsum", [P, E], BF16)
        key0 = sb("key0", [P, E])
        key = sb("key", [P, E])
        key8 = sb("key8", [P, 8])
        wraw = sb("wraw", [P, TOPK])
        wjunk = sb("wjunk", [P, TOPK, E])
        slot_ix = sb("slot_ix", [P, 2, TOPK], I32)
        late = x_sb[:, :, 2:4, :].rearrange("p b g d -> p b (g d)")
        sth, sht = late[:, 0:2, :], late[:, 2:6, :].rearrange("p (t m) n -> p t m n", t=2)
        cnt_i = sb("cnt_i", [E, 2], I32)
        nt_f = sb("nt_f", [E, 3])
        nt_b = sb("nt_b", [E, 1], BF16)
        cum = sb("cum", [E, 1])
        past = sb("past", [E, NTAB])
        pad_ix = sb("pad_ix", [1, E], I32)
        tab = sb("tab", [1, 4, NTAB])
        tabf = sb("tabf", [1, NTAB + 1])
        tab_i = sb("tab_i", [1, NTAB, 4], I32)
        rank_i = sb("rank_i", [1, NTAB], I32)
        slot_i = sb("slot_i", [1, NTAB + U], I32)
        turn_slots = sb("turn_slots", [1, TURNS + 1, SLOTS_AT], I32)
        live = sb("live", [1, TURNS + 1])
        last_turn = sb("last_turn", [1, 1], I32)
        myslot = sb("myslot", [P, NTAB])
        wring = sb("wring", [P, RING, WCOLS])
        free = kmask[:].rearrange("p t h k -> p (t h k)")
        xring = free[:, 0:U * ROW].rearrange("p (r n) -> p r n", n=ROW)
        y = free[:, U * ROW:U * ROW + NACC * D].rearrange("p (a n) -> p a n", n=D)
        spare = wring[:].rearrange("p r n -> p (r n)")
        junk, zeros = spare[:, 0:NG * D], spare[:, NG * D:NG * D + 1024]
        flat = x_sb[:].rearrange("p b g d -> p (b g d)")
        xt = prob[:, :, 0:KT, :]
        silu, hm, ht = probt[:, :, 0, :], probt[:, :, 1, :], probt[:, :, 2, :]
        wtile = sb("wtile", [P, U, 1])
        token_ix = sb("token_ix", [P, U, 1], I32)
        wtj = sb("wtj", [P, U, TOPK])

        ps = [psum(f"ps{i}") for i in range(8)]
        psS, psT, psO, psA, psX, psC = ps[0:2], ps[2:4], ps[4], ps[5], ps[6], ps[7]
        psG, psU, psD = ps[0:2], ps[2:4], ps[4:6]

        s = {}

        def S(name):
            if name not in s:
                s[name] = sem(name)
            return s[name]

        weights_in = [S(f"weights_in{i}") for i in range(15)]
        const_in = S("const_in")
        x_in = [S(f"x_in{i}") for i in range(7)]
        for name in ("consts_ready", "zeros_ready", "sum_act", "sum_dve", "tok_chain", "tok_hid", "tok_tanh", "tok_h",
                     "tok_w", "tok_shift", "tok_exp", "tok_ready",
                     "mix_chain", "ln1_done", "xn_transposed", "xnt_ready", "qk_done",
                     "q_ready", "k_ready", "kmask_ready", "v_done", "v_ready",
                     "scores_done", "max_done", "nmax_ready", "exp_done", "prob_transposed", "probt_ready",
                     "pv_done", "ot_ready", "ot_turned", "c2_chain", "o_ready", "o_transposed", "ont_ready",
                     "bias_added", "proj_done", "ln_chain", "x2_ready", "x2_transposed", "x2t_ready",
                     "gate_done", "gate_tanh", "g_chain", "score_read", "sel_ready", "pos_done", "key_read", "d_chain",
                     "pool_step", "gu_done", "gu_tanh", "sh_chain", "sh_mul", "shared_done", "h2_ready",
                     "row_ready",
                     "t_chain", "t_count", "t_cum", "t_past", "t_rows", "t_rowf", "t_bcast", "tab_ready",
                     "pad_ready", "myslot_ready",
                     "xt_done", "xt_ready", "up_done", "silu_done", "h_ready", "h_turned", "ht_ready",
                     "down_done", "wt_done", "y_ready", "fin_chain", "fin_ready"):
            S(name)
        scattered = [S(f"scattered{i}") for i in range(2)]
        acc_zero = S("acc_zero")
        padded = [S(f"padded{k}") for k in range(2)]
        w_in = [S(f"w_in{q}") for q in range(U)]
        xt_in = [S(f"xt_in{q}") for q in range(U)]
        added = [S(f"added{a}") for a in range(NACC)]
        stored = S("stored")

        FIN = 2
        CH = FIN * D
        fin_in = [S(f"fin_in{j}") for j in range(NB // FIN)]
        NCH = TOKENS * D // P // CH
        fin_sb = flat[:, 0:NACC * TOKENS * D // P].rearrange("p (i a n) -> p i a n", a=NACC, n=CH)

        block = ctx.enter_context(nc.Block())

        def image_loop(eng, step, first, last):
            for b in range(first, 4):
                step(b, b % 2)
            with eng.Fori(2, 6) as i:
                for par in range(2):
                    step(2 * i + par, par)
            for b in range(12, last + 1):
                step(b, b % 2)

        PARTS = ((0, 4), (4, NB))
        ACT_SUMS = {-3: (0, 2), -2: (4, 5), -1: (6, 7, 8), 0: (9, 10, 12, 14)}
        DVE_SUMS = {-3: (1, 3), 0: (11, 13, 15)}
        TABLES = 5

        def has(b, lo=0, hi=NB - 1):
            return not isinstance(b, int) or lo <= b <= hi

        def tile_loop(eng, engine, step, first, drain):
            for t in range(first, U):
                step(0, t, t, False)
            last = eng.value_load(last_turn[0:1, 0:1], min_val=0, max_val=TURNS - 1)
            with eng.Fori(1, TURNS) as i:
                with eng.If(i < last + 1):
                    for q in range(U):
                        step(i, q, U * i + q, False)
            for q in range(drain):
                step(last + 1, q, U * last + (U + q), True)
            return last

        def loaded(src, engine, most):
            why = "the table's making bounds it for any counts"
            _, vals = nc.values_load_multi_w_load_instructions(src, engines=[engine], min_val=0, max_val=max(most),
                                                               skip_runtime_bounds_check_because=why)
            return [nc.s_assert_within(v, 0, m, skip_runtime_bounds_check_because=why)
                    for v, m in zip(vals, most)]

        SP_PADS = 40

        def pad_rows(eng, engine, e):
            for at in loaded(pad_ix[0:1, e:e + 4], engine, (SLOTS - P,) * 4):
                eng.dma_start(slots_dram[ds(at, P), :], c("pad")).then_inc(padded[engine == SCALAR], 16)

        @block.sync
        def _(sp):
            for j in range(4):
                sp.dma_start(x_sb[:, j, :, :], x[j].rearrange("g c d -> c g d")).then_inc(x_in[j], 16)
                if j == 0:
                    sp.dma_start(w1_sb[:], w1t).then_inc(weights_in[0], 16)
                    sp.dma_start(b1_sb[:], b1).then_inc(weights_in[1], 16)
            sp.dma_start(w2_sb[:], w2t).then_inc(weights_in[2], 16)
            sp.dma_start(b2_sb[:], b2).then_inc(weights_in[3], 16)
            sp.dma_start(const_sb[:], const).then_inc(const_in, 16)
            sp.dma_start(wqkv_sb[:], wqkv).then_inc(weights_in[4], 16)
            sp.dma_start(bqk_sb[:], bqk).then_inc(weights_in[5], 16)
            sp.dma_start(bv_sb[:], bv.to_broadcast([P, D])).then_inc(weights_in[6], 16)
            sp.dma_start(bo_sb[:], bo.to_broadcast([P, D])).then_inc(weights_in[8], 16)
            for j in range(1, 4):
                sp.dma_start(x_sb[:, 4 * j:4 * j + 4, :, :].rearrange("p b g d -> p (b g) d"),
                             x[4 * j:4 * j + 4].rearrange("b g c d -> c (b g) d")).then_inc(x_in[3 + j], 16)
            sp.dma_start(wo_sb[:], wo).then_inc(weights_in[7], 16)
            sp.dma_start(gbias_sb[:], gbias.to_broadcast([P, E])).then_inc(weights_in[9], 16)
            sp.dma_start(gate_sb[:], gate).then_inc(weights_in[10], 16)
            sp.dma_start(sgu_sb[:], sgu).then_inc(weights_in[11], 16)
            sp.dma_start(sd_sb[:], sd).then_inc(weights_in[12], 16)
            sp.wait_ge(const_in, 16)
            sp.wait_ge(S("zeros_ready"), 1)
            for a in range(NACC):
                for j in range(4):
                    sp.dma_start(acc_dram[a][j * 512:(j + 1) * 512, :].rearrange("(p n) d -> p (n d)", p=P),
                                 zeros).then_inc(acc_zero, 16)
                sp.dma_start(acc_dram[a][TOKENS:TOKENS + P, :], zeros[:, 0:D]).then_inc(acc_zero, 16)
            sp.dma_start(slots_dram[SLOTS:SLOTS + P, :], c("pad")).then_inc(acc_zero, 16)

            sp.wait_ge(S("pad_ready"), 1)
            for e in range(0, SP_PADS, 4):
                pad_rows(sp, SP, e)
            sp.wait_ge(padded[0], 16 * SP_PADS)
            sp.wait_ge(padded[1], 16 * (E - SP_PADS))
            sp.wait_ge(acc_zero, 16 * (NACC * 5 + 1))
            for par in range(2):
                sp.wait_ge(scattered[par], 16 * TOPK * NB // 2)
            sp.wait_ge(S("tab_ready"), TABLES)

            def load_tile(i, q, t, tail):
                u, uq, turn = t + 1, (q + 1) % U, i + (q + 1) // U
                at, slot, ex, fresh = loaded(tab_i[0:1, ds(u, 1), :].rearrange("p a b -> p (a b)"), SP,
                                             (SLOTS, RING - 1, E - 1, 1))
                wait(sp, S("down_done"), u - RING + 1)
                sp.dma_start(wring[:, ds(slot, 1), :], wexp[ds(ex, 1)].rearrange("a p d -> p a d"),
                             cond=fresh).then_inc(w_in[uq], 16)
                wait(sp, S("wt_done"), u - U + 1)
                sp.dma_start(xring[:, uq, :], slots_dram[ds(at, P), :]).then_inc(xt_in[uq], 16)
            last = tile_loop(sp, SP, load_tile, -1, 0)
            sp.wait_ge(xt_in[0], 16 * last + 32)
            sp.wait_ge(w_in[0], 16 * last + 32)

            for a in range(NACC):
                sp.wait_ge(added[a], 16 * (U // NACC) * last + 16 * (U // NACC))
            for j in range(NCH):
                for a in range(NACC):
                    sp.dma_start(fin_sb[:, j, a, :].rearrange("p (n d) -> p n d", d=D),
                                 acc_dram[a][j * FIN * P:(j + 1) * FIN * P, :].rearrange(
                                     "(n p) d -> p n d", p=P)).then_inc(fin_in[j], 16)

        @block.gpsimd
        def _(pool):
            nc.gpsimd.memset(zeros, 0.0).then_inc(S("zeros_ready"), 1)
            pool.wait_ge(const_in, 16)

            pool.wait_ge(weights_in[8], 16)

            def step(b, par):
                v, a, d = b + 1, b + 2, b - 3
                if has(v):
                    pool.wait_ge(S("ln1_done"), v + 1)
                    hb = h_all[:, ds(v, 1), :].rearrange("p a d -> p (a d)")
                    nc.gpsimd.tensor_tensor(hb, hb, bo_sb[:], ALU.add).then_inc(S("bias_added"), 1)
                if has(d):
                    pool.wait_ge(S("row_ready"), d + 1)
                    pool.sem_inc(S("pool_step"), 1)
                    for k in range(TOPK):
                        nc.gpsimd.indirect_dma_start(
                            out=slots_dram,
                            out_offset=bass.IndirectOffsetOnAxis(ap=slot_ix[:, 1 - par, k:k + 1], axis=0),
                            in_=row[:, 1 - par, :], in_offset=None).then_inc(scattered[1 - par], 16)
                if has(a):
                    pool.wait_ge(S("k_ready"), 2 * a + 2)
                    wait(pool, S("scores_done"), NGRP * (a - 1))
                    for m in range(2):
                        nc.gpsimd.tensor_tensor(
                            kmask[:, par, 8 * m:8 * m + 8, :],
                            kt[:, par, m, :].unsqueeze(1).to_broadcast([P, 8, P]),
                            c("head").unsqueeze(2).to_broadcast([P, 8, P]), ALU.mult).then_inc(S("kmask_ready"), 1)
            image_loop(pool, step, -2, NB + 2)

            pool.wait_ge(S("tab_ready"), TABLES)

            def add_tile(i, q, t, tail):
                a = q % NACC
                turn = U // NACC * i + q // NACC
                pool.wait_ge(S("y_ready"), t + 1)
                wait(pool, added[a], 16 * turn)
                pool.sem_inc(S("pool_step"), 1)
                nc.gpsimd.indirect_dma_start(
                    out=acc_dram[a],
                    out_offset=bass.IndirectOffsetOnAxis(ap=token_ix[:, q, :], axis=0),
                    in_=y[:, a, :], in_offset=None, compute_op=ALU.add).then_inc(added[a], 16)
            tile_loop(pool, POOL, add_tile, 0, 0)

        @block.scalar
        def _(act):
            summed = [0]

            def sum_image(b):
                act.wait_ge(x_in[min(b, 3 + b // 4)], 16)
                if summed[0]:
                    act.wait_ge(S("sum_act"), summed[0])
                summed[0] += 1
                nc.scalar.activation(junk, x_sb[:, b, :, :].rearrange("p g d -> p (g d)"), ACT.Identity,
                                     accum_out=xsum[:, b:b + 1]).then_inc(S("sum_act"), 1)

            def mixing_tanh(part):
                lo, hi = PARTS[part]
                act.wait_ge(S("tok_hid"), 2 * part + 1)
                nc.scalar.activation(gel[:, 3, lo:hi], gel[:, 2, lo:hi], ACT.Tanh, scale=0.7978845608028654).then_inc(
                    S("tok_tanh"), 1)

            def mixing_exp(part):
                lo, hi = PARTS[part]
                act.wait_ge(S("tok_shift"), part + 1)
                nc.scalar.activation(wexpd[:, lo:hi, :], wshift[:, lo:hi, :], ACT.Exp).then_inc(S("tok_exp"), 1)

            for img in ACT_SUMS[-3]:
                sum_image(img)
            mixing_tanh(0)
            mixing_exp(0)
            act.wait_ge(weights_in[5], 16)

            def shared_tanh(j):
                for m in range(2):
                    act.wait_ge(S("gu_done"), 4 * j + m + 1)
                    wait(act, S("sh_chain"), 2 * (j - 1) + m + 1)
                    nc.scalar.activation(sth[:, m, :], psG[m][:], ACT.Tanh, scale=0.5).then_inc(S("gu_tanh"), 1)

            def step(b, par):
                a, cc, d, q = b + 2, b - 1, b - 2, 1 - par
                if isinstance(b, int) and b in ACT_SUMS:
                    for img in ACT_SUMS[b][0:3 if b else 2]:
                        sum_image(img)
                if isinstance(b, int) and b == 1:
                    mixing_exp(1)

                def exp(img, g):
                    n, sp = NGRP * img + g, g % 2
                    act.wait_ge(S("nmax_ready"), n + 1)
                    wait(act, S("prob_transposed"), n - 1)
                    for j in range(GH):
                        last = nc.scalar.activation(prob[:, sp, j, :], psS[sp][:, j * P:(j + 1) * P], ACT.Exp,
                                                    bias=nmax[:, sp, j:j + 1], scale=HD ** -0.5)
                    last.then_inc(S("exp_done"), 1)

                def turn(g):
                    n, sp = NGRP * b + g, g % 2
                    act.wait_ge(S("prob_transposed"), n + 1)
                    wait(act, S("pv_done"), n - 1)
                    nc.scalar.copy(probt[:, sp].rearrange("p a k -> p (a k)"), psT[sp][:]).then_inc(
                        S("probt_ready"), 1)

                def project(m, dst, ready):
                    nc.scalar.activation(dst[:, par, m % 2, :], psA[:, m * P:(m + 1) * P], ACT.Identity,
                                         bias=bqk_sb[:, m:m + 1]).then_inc(S(ready), 1)

                if has(b):
                    turn(0)
                    exp(b, 1)
                    turn(1)
                    exp(b, 2)
                if isinstance(b, int) and b == 0:
                    for img in ACT_SUMS[0][2:]:
                        sum_image(img)
                if has(d):
                    act.wait_ge(S("x2_transposed"), d + 1)
                    wait(act, S("gate_done"), d)
                    nc.scalar.copy(x2t[:].rearrange("p a k -> p (a k)"), psX[:, 0:D]).then_inc(S("x2t_ready"), 1)
                if has(cc):
                    act.wait_ge(S("o_transposed"), cc + 1)
                    wait(act, S("proj_done"), cc)
                    nc.scalar.copy(ont[:].rearrange("p a k -> p (a k)"), psC[:, 0:D]).then_inc(S("ont_ready"), 1)
                if has(d):
                    nc.scalar.copy(x_sb[:, ds(d, 1), 1, :].rearrange("p a d -> p (a d)"), psX[:, 0:D]).then_inc(
                        S("x2t_ready"), 1)
                if has(a):
                    act.wait_ge(S("xn_transposed"), a + 1)
                    wait(act, S("v_done"), a - 1)
                    nc.scalar.copy(xnt[:, par].rearrange("p a k -> p (a k)"), psA[:, 0:D]).then_inc(
                        S("xnt_ready"), 1)
                if has(b):
                    turn(2)
                if has(d):
                    act.wait_ge(S("gate_done"), d + 1)
                    wait(act, S("score_read"), d)
                    nc.scalar.activation(gth[:], psX[:, 0:E], ACT.Tanh, scale=0.5).then_inc(S("gate_tanh"), 1)
                if has(b):
                    exp(b, 3)
                if has(a):
                    act.wait_ge(S("qk_done"), 2 * a + 1)
                    wait(act, S("kmask_ready"), 2 * (a - 1))
                    for m in (2, 3):
                        project(m, kt, "k_ready")
                if has(b):
                    turn(3)
                if has(b + 1):
                    exp(b + 1, 0)
                if isinstance(b, int) and b == 0:
                    mixing_tanh(1)
                if has(b):
                    act.wait_ge(S("pv_done"), NGRP * (b + 1))
                    wait(act, S("ot_turned"), b)
                    nc.scalar.copy(ot_sb[:].rearrange("p a k -> p (a k)"), psO[:]).then_inc(S("ot_ready"), 1)
                if has(a):
                    act.wait_ge(S("qk_done"), 2 * a + 2)
                    wait(act, S("scores_done"), NGRP * (a - 1))
                    for m in (0, 1):
                        project(m, qt, "q_ready")
                if isinstance(b, int) and b == NB + 1:
                    shared_tanh(0)
            image_loop(act, step, -2, NB + 1)

            act.wait_ge(S("pad_ready"), 1)
            for j in range(1, 4):
                for e in range(SP_PADS + 8 * (j - 1), SP_PADS + 8 * j, 4):
                    pad_rows(act, SCALAR, e)
                shared_tanh(j)

            act.wait_ge(S("tab_ready"), TABLES)
            nc.scalar.activation(silu[:, 0, :], silu[:, 1, :], ACT.Silu)

            def tile_step(i, q, t, tail):
                u = t + 1
                if not tail:
                    act.wait_ge(S("xt_done"), u + 1)
                    wait(act, S("up_done"), u - 1)
                    nc.scalar.copy(xt[:, (q + 1) % 2].rearrange("p a k -> p (a k)"),
                                   psT[(q + 1) % 2][:, 0:D]).then_inc(S("xt_ready"), 1)
                if has(t, 0, NT) and not tail:
                    act.wait_ge(S("up_done"), t + 1)
                    wait(act, S("h_ready"), t - 1)
                    nc.scalar.activation(silu[:, q % 2, :], psS[q % 2][:, 0:INTER], ACT.Silu).then_inc(
                        S("silu_done"), 1)
                if has(t - 1, 0, NT):
                    act.wait_ge(S("h_turned"), t)
                    wait(act, S("down_done"), t - 2)
                    nc.scalar.copy(ht[:, (q + 1) % 2, :], ps[4 + (q + 1) % 2][:, 0:P]).then_inc(S("ht_ready"), 1)
            tile_loop(act, SCALAR, tile_step, -1, 1)

            for j in range(NCH):
                act.wait_ge(S("fin_ready"), j + 1)
                act.dma_start(out[j * FIN * P:(j + 1) * FIN * P, :].rearrange("(n p) d -> p n d", p=P),
                              fin_sb[:, j, 0, :].rearrange("p (n d) -> p n d", d=D)).then_inc(stored, 16)
            act.wait_ge(stored, 16 * NCH)

        @block.vector
        def _(dve):
            tok = [0]

            def link(ins, chain, base, count):
                count[0] += 1
                ins.then_inc(S(chain), 1)
                dve.wait_ge(S(chain), base + count[0])

            def start(chain):
                dve.sem_clear(S(chain))
                return [0]

            nc.vector.memset(ones_b[:], 1.0)
            nc.vector.memset(ones_f[:], 1.0)
            nc.vector.memset(selsum[:], 0.0)
            nc.vector.memset(gmx[:, EG:], BIG)
            nc.vector.memset(masked[:, :, E:], BIG)
            nc.vector.memset(vaug[:, :, :, HD + 1:], 0.0)
            nc.vector.memset(nt_f[:, 0:1], 1.0)
            nc.vector.memset(tabf[:, 0:1], -1.0)
            nc.vector.memset(slot_i[:], 0)
            nc.vector.memset(turn_slots[:], 0)
            nc.vector.memset(vaug[:, :, :, HD:HD + 1], 1.0)

            def sum_image(b):
                dve.wait_ge(x_in[min(b, 3 + b // 4)], 16)
                nc.vector.reduce_sum(xsum[:, b:b + 1], x_sb[:, b, :, :].rearrange("p g d -> p (g d)"),
                                     axis=AX).then_inc(S("sum_dve"), 1)

            def lk(ins):
                link(ins, "tok_chain", 0, tok)

            def hidden(part):
                lo, hi = PARTS[part]
                n, at = hi - lo, psC if part else psA
                dve.wait_ge(weights_in[1], 16)
                dve.wait_ge(S("tok_h"), part + 1)
                g = [gel[:, k, lo:hi] for k in range(5)]
                lk(nc.vector.tensor_scalar(g[0], at[0:HID, 0:n], 1.0 / D, b1_sb[:, 0:1], ALU.mult, ALU.add))
                lk(nc.vector.tensor_tensor(g[1], g[0], g[0], ALU.mult))
                lk(nc.vector.tensor_scalar(g[1], g[1], 0.044715, 1.0, ALU.mult, ALU.add))
                nc.vector.tensor_tensor(g[2], g[0], g[1], ALU.mult).then_inc(S("tok_hid"), 1)
                if part == 0:
                    dve.wait_ge(const_in, 16)
                    nc.vector.tensor_copy(ident_b[:], ident)
                    for k in range(GH):
                        nc.vector.tensor_copy(causal_b[:, k, :], c("causal"))
                    nc.vector.tensor_copy(before_b[:], c("before"))
                    nc.vector.tensor_copy(upto_b[:], c("upto", E)).then_inc(S("consts_ready"), 1)

            def gelu(part):
                lo, hi = PARTS[part]
                g = [gel[:, k, lo:hi] for k in range(5)]
                dve.wait_ge(S("tok_tanh"), part + 1)
                nc.vector.scalar_tensor_tensor(out=g[4], in0=g[3], scalar=1.0, in1=g[0],
                                               op0=ALU.add, op1=ALU.mult).then_inc(S("tok_hid"), 1)

            def weights(part):
                lo, hi = PARTS[part]
                n, at = hi - lo, psC if part else psA
                dve.wait_ge(S("tok_w"), part + 1)
                dve.wait_ge(weights_in[3], 16)
                lk(nc.vector.scalar_tensor_tensor(
                    out=wtok[:, lo:hi, :], in0=at[:, 0:NG * n].rearrange("p (g b) -> p b g", g=NG), scalar=0.5,
                    in1=b2_sb[:].unsqueeze(1).to_broadcast([P, n, NG]), op0=ALU.mult, op1=ALU.add))
                lk(nc.vector.tensor_reduce(wsm[:, 0, lo:hi], wtok[:, lo:hi, :], axis=AX, op=ALU.max))
                nc.vector.tensor_tensor(wshift[:, lo:hi, :], wtok[:, lo:hi, :],
                                        wsm[:, 0, lo:hi].unsqueeze(2).to_broadcast([P, n, NG]),
                                        ALU.subtract).then_inc(S("tok_shift"), 1)
                dve.wait_ge(S("tok_exp"), part + 1)
                lk(nc.vector.tensor_reduce(wsm[:, 1, lo:hi], wexpd[:, lo:hi, :], axis=AX, op=ALU.add))
                lk(nc.vector.reciprocal(wsm[:, 2, lo:hi], wsm[:, 1, lo:hi]))
                lk(nc.vector.tensor_tensor(wtok[:, lo:hi, :], wexpd[:, lo:hi, :],
                                           wsm[:, 2, lo:hi].unsqueeze(2).to_broadcast([P, n, NG]), ALU.mult))

            for img in DVE_SUMS[-3]:
                sum_image(img)
            hidden(0)
            gelu(0)
            weights(0)

            def image(t, img):
                return t[:, ds(img, 1), :].rearrange("p a d -> p (a d)")

            def mix(a, g):
                hb = image(h_all, a)
                xg = x_sb[:, ds(a, 1), g, :].rearrange("p a d -> p (a d)")
                wg = wtok[:, ds(a, 1), g:g + 1].rearrange("p a d -> p (a d)")
                if g == 0:
                    dve.sem_clear(S("mix_chain"))
                    nc.vector.tensor_scalar(hb, xg, wg, None, ALU.mult).then_inc(S("mix_chain"), 1)
                    return
                dve.wait_ge(S("mix_chain"), g)
                nc.vector.scalar_tensor_tensor(out=hb, in0=xg, scalar=wg, in1=hb, op0=ALU.mult,
                                               op1=ALU.add).then_inc(S("mix_chain"), 1)

            ROOT = 11

            def root(k, lo, hi, base):
                v, y, r, z = (rs[:, n, lo:hi] for n in range(4))
                dve.wait_ge(S("ln_chain"), base + k)

                def done(ins):
                    ins.then_inc(S("ln_chain"), 1)
                if k == 0:
                    done(nc.vector.tensor_scalar(v, mv[:, lo:hi, 1], EPS, None, ALU.add))
                elif k == 1:
                    done(nc.vector.tensor_single_scalar(z.bitcast(I32), v.bitcast(I32), 1, ALU.arith_shift_right))
                elif k == 2:
                    done(nc.vector.tensor_scalar(y.bitcast(I32), z.bitcast(I32), -1.0, float(0x5F3759DF), ALU.mult,
                                                 ALU.add))
                elif k in (3, 8):
                    done(nc.vector.tensor_tensor(r, y, y, ALU.mult))
                elif k in (4, 9):
                    done(nc.vector.tensor_tensor(r, r, v, ALU.mult))
                elif k == 5:
                    done(nc.vector.tensor_scalar(z, r, 0.375, -1.25, ALU.mult, ALU.add))
                elif k == 6:
                    done(nc.vector.tensor_tensor(z, z, r, ALU.mult))
                elif k == 7:
                    done(nc.vector.scalar_tensor_tensor(out=y, in0=z, scalar=1.875, in1=y, op0=ALU.add,
                                                        op1=ALU.mult))
                elif k == 10:
                    done(nc.vector.tensor_scalar(z, r, -0.5, 1.5, ALU.mult, ALU.add))
                elif k == ROOT:
                    done(nc.vector.tensor_tensor(y, y, z, ALU.mult))

            def apply(src, dst, which):
                return nc.vector.tensor_scalar(dst, src, mv[:, which, 0:1], rs[:, 1, which:which + 1],
                                               ALU.subtract, ALU.mult)

            def smax_of(b, g):
                n, sp = NGRP * b + g, g % 2
                dve.wait_ge(S("scores_done"), n + 1)
                nc.vector.tensor_reduce(smax[:, sp, :], psS[sp][:].rearrange("p (a k) -> p a k", a=GH), axis=AX,
                                        op=ALU.max).then_inc(S("max_done"), 1)

            def nmax_of(b, g):
                n, sp = NGRP * b + g, g % 2
                dve.wait_ge(S("max_done"), n + 1)
                wait(dve, S("exp_done"), n - 1)
                nc.vector.tensor_scalar(nmax[:, sp, :], smax[:, sp, :], -HD ** -0.5, None, ALU.mult).then_inc(
                    S("nmax_ready"), 1)

            def v_evac(a, q):
                dve.wait_ge(S("v_done"), a + 1)
                wait(dve, S("pv_done"), NGRP * (a - 1))
                nc.vector.tensor_tensor(vaug[:, q, :, 0:HD], psA[:, 0:D].rearrange("p (h d) -> p h d", d=HD),
                                        bv_sb[:].rearrange("p (h d) -> p h d", d=HD), ALU.add).then_inc(
                    S("v_ready"), 1)

            o3 = psX[:].rearrange("p (h d) -> p h d", d=2 * HD)

            def den_of(cc):
                dve.wait_ge(S("ot_turned"), cc + 1)
                nc.vector.reciprocal(rden[:], o3[:, :, HD:HD + 1].rearrange("p h o -> p (h o)")).then_inc(
                    S("c2_chain"), 1)

            def normalise(cc):
                dve.wait_ge(S("c2_chain"), cc + 1)
                wait(dve, S("o_transposed"), cc)
                nc.vector.tensor_tensor(o_sb[:].rearrange("p (h d) -> p h d", d=HD), o3[:, :, 0:HD],
                                        rden[:].unsqueeze(2).to_broadcast([P, HEADS, HD]), ALU.mult).then_inc(
                    S("o_ready"), 1)

            ROUTE = 12

            def route(d, q, k):
                if k == 0:
                    dve.sem_clear(S("g_chain"))
                    dve.wait_ge(S("gate_tanh"), d + 1)
                    nc.vector.scalar_tensor_tensor(out=score[:], in0=gth[:], scalar=0.5, in1=gbias_half[:],
                                                   op0=ALU.mult, op1=ALU.add).then_inc(S("score_read"), 1)
                    return
                if k == 1:
                    dve.wait_ge(S("score_read"), d + 1)
                else:
                    dve.wait_ge(S("g_chain"), k - 1)
                mk = masked[:, q, :]

                def done(ins):
                    ins.then_inc(S("g_chain"), 1)
                if k == 1:
                    done(nc.vector.tensor_reduce(gmx[:, 0:EG], score[:].rearrange("p (g e) -> p g e", g=EG),
                                                 axis=AX, op=ALU.max))
                elif k == 2:
                    done(nc.vector.max(gmx8[:], gmx[:]))
                elif k == 3:
                    done(nc.vector.match_replace(gmr[:], gmx8[:], gmx[:], -BIG))
                elif k == 4:
                    done(nc.vector.tensor_scalar(gsel[:], gmr[:, 0:EG], -BIG, None, ALU.is_equal))
                elif k == 5:
                    done(nc.vector.tensor_tensor(mk[:, 0:E].rearrange("p (g e) -> p g e", g=EG),
                                                 score[:].rearrange("p (g e) -> p g e", g=EG),
                                                 gsel[:].unsqueeze(2).to_broadcast([P, EG, EG]), ALU.mult))
                elif k == 6:
                    done(nc.vector.max(top8[:], mk))
                elif k == 7:
                    done(nc.vector.match_replace(topr[:], top8[:], mk, -BIG))
                elif k == 8:
                    nc.vector.tensor_scalar(sel_b[:, q, :], topr[:, 0:E], -BIG, None, ALU.is_equal).then_inc(
                        S("sel_ready"), 1)
                    done(nc.vector.reduce_sum(tsum[:], top8[:, 2:8], axis=AX))
                elif k == 9:
                    done(nc.vector.tensor_scalar(tsum[:], tsum[:], 1e-8, None, ALU.add))
                elif k == 10:
                    done(nc.vector.reciprocal(tinv[:, q:q + 1], tsum[:]))
                elif k == 11:
                    done(nc.vector.tensor_copy(row[:, q, ID_AT:ID_AT + 1].bitcast(I32),
                                               c("ids")[:, ds(d, 1)].bitcast(I32)))
                elif k == ROUTE:
                    pass

            def place(d, q, k):
                if k == 0:
                    dve.sem_clear(S("d_chain"))
                    dve.wait_ge(S("pos_done"), d + 1)
                    nc.vector.tensor_tensor(key0[:], psC[:, 0:E], c("ebase"), ALU.add).then_inc(S("key_read"), 1)
                    nc.vector.tensor_tensor(selsum[:], selsum[:], sel_b[:, q, :], ALU.add).then_inc(
                        S("d_chain"), 1)
                elif k == 1:
                    dve.wait_ge(S("key_read"), d + 1)
                    nc.vector.tensor_tensor(key[:], key0[:], sel_b[:, q, :], ALU.mult).then_inc(S("d_chain"), 1)
                elif k == 2:
                    dve.wait_ge(S("d_chain"), 2)
                    nc.vector.max(key8[:], key[:]).then_inc(S("d_chain"), 1)
                elif k == 3:
                    dve.wait_ge(S("d_chain"), 3)
                    nc.vector.tensor_scalar(slot_ix[:, q, :], key8[:, 0:TOPK], 1.0, None, ALU.subtract)
                    nc.vector.tensor_scalar(row[:, q, S_AT:S_AT + TOPK], key8[:, 0:TOPK], 1.0, None, ALU.subtract)
                elif k == 4:
                    for n in range(TOPK):
                        nc.vector.scalar_tensor_tensor(
                            out=wjunk[:, n, :], in0=key[:], scalar=key8[:, n:n + 1], in1=masked[:, q, 0:E],
                            op0=ALU.is_equal, op1=ALU.mult, accum_out=wraw[:, n:n + 1]).then_inc(S("d_chain"), 1)
                elif k == 5:
                    dve.wait_ge(S("d_chain"), 3 + TOPK)
                    nc.vector.tensor_scalar(row[:, q, W_AT:W_AT + TOPK], wraw[:], tinv[:, q:q + 1], None,
                                            ALU.mult).then_inc(S("row_ready"), 1)

            dve.wait_ge(weights_in[6], 16)

            def shared_gate(j):
                for m in range(2):
                    dve.wait_ge(S("gu_tanh"), 2 * j + m + 1)
                    nc.vector.scalar_tensor_tensor(out=sth[:, m, :], in0=sth[:, m, :], scalar=1.0, in1=psG[m][:],
                                                   op0=ALU.add, op1=ALU.mult).then_inc(S("sh_mul"), 1)

            def shared_mul(j):
                for m in range(2):
                    dve.wait_ge(S("gu_done"), 4 * j + 3 + m)
                    dve.wait_ge(S("sh_mul"), 2 * j + m + 1)
                    wait(dve, S("shared_done"), 4 * (j - 1))
                    nc.vector.scalar_tensor_tensor(out=sht[:, j % 2, m, :], in0=sth[:, m, :], scalar=0.5,
                                                   in1=psU[m][:], op0=ALU.mult, op1=ALU.mult).then_inc(
                        S("sh_chain"), 1)

            def shared_out(j):
                for n in range(4):
                    hb = h_all[:, 4 * j + n, :]
                    dve.wait_ge(S("shared_done"), 4 * j + n + 1)
                    nc.vector.tensor_tensor(hb, hb, psD[n % 2][:, 0:D], ALU.add).then_inc(S("h2_ready"), 1)

            def step(b, par):
                a, v, cc, d, e, q = b + 3, b + 1, b - 1, b - 2, b - 3, 1 - par
                first = isinstance(b, int) and b == -1
                if isinstance(b, int) and b == 1:
                    weights(1)
                    dve.wait_ge(weights_in[9], 16)
                    lk(nc.vector.tensor_scalar(gbias_half[:], gbias_sb[:], 0.5, None, ALU.add))
                if has(e):
                    place(e, q, 0)
                if has(cc):
                    den_of(cc)
                if has(e):
                    place(e, q, 1)
                if has(cc):
                    normalise(cc)
                if has(e):
                    place(e, q, 2)
                if has(b):
                    smax_of(b, 2)
                if has(e):
                    place(e, q, 3)
                if has(b):
                    nmax_of(b, 2)
                if has(e):
                    place(e, q, 4)
                if has(a):
                    mix(a, 0)
                if has(e):
                    place(e, q, 5)
                if has(v) and not first:
                    v_evac(v, q)
                if has(a):
                    mix(a, 1)
                if has(b):
                    smax_of(b, 3)
                if has(a):
                    mix(a, 2)
                if has(b):
                    nmax_of(b, 3)
                if isinstance(b, int) and b == 0:
                    for img in DVE_SUMS[0]:
                        sum_image(img)
                    hidden(1)
                if has(a):
                    mix(a, 3)

                lo, hi = 0 if has(a) else 1, 2 if has(cc) else 1
                ln = [0]

                def norm_step(ins):
                    ins.then_inc(S("ln_chain"), 1)
                    ln[0] += 1
                if hi > lo:
                    dve.sem_clear(S("ln_chain"))
                if has(d):
                    route(d, par, 0)
                if has(a):
                    dve.wait_ge(S("mix_chain"), NG)
                    norm_step(nc.vector.bn_stats(st[:, 0, :], image(h_all, a)))
                if first:
                    v_evac(v, q)
                if has(d):
                    route(d, par, 1)
                if has(v):
                    smax_of(v, 0)
                if has(d):
                    route(d, par, 2)
                if has(v):
                    nmax_of(v, 0)
                if has(d):
                    route(d, par, 3)
                    route(d, par, 4)
                if has(cc):
                    dve.wait_ge(S("proj_done"), cc + 1)
                    dve.wait_ge(S("bias_added"), cc + 1)
                    norm_step(nc.vector.tensor_tensor(image(h_all, cc), image(h_all, cc), psC[:, D:2 * D], ALU.add))
                if has(d):
                    route(d, par, 5)
                if has(cc):
                    dve.wait_ge(S("ln_chain"), ln[0])
                    norm_step(nc.vector.bn_stats(st[:, 1, :], image(h_all, cc)))
                if has(d):
                    route(d, par, 6)
                at = ln[0]
                for w in range(lo, hi):
                    dve.wait_ge(S("ln_chain"), at)
                    norm_step(nc.vector.bn_aggr(mv[:, w, :], st[:, w, :]))
                at = ln[0]
                for k in range(ROOT + 1):
                    if has(d) and k + 7 <= ROUTE:
                        route(d, par, k + 7)
                    if hi > lo:
                        root(k, lo, hi, at)
                    if has(v) and k == 7:
                        smax_of(v, 1)
                    if has(v) and k == 9:
                        nmax_of(v, 1)
                if has(cc):
                    dve.wait_ge(S("ln_chain"), at + ROOT + 1)
                    wait(dve, scattered[q], 8 * TOPK * (cc - q))
                    apply(image(h_all, cc), row[:, q, 0:D], 1).then_inc(S("x2_ready"), 1)
                if has(a):
                    dve.wait_ge(S("ln_chain"), at + ROOT + 1)
                    wait(dve, S("xn_transposed"), a - 1)
                    apply(image(h_all, a), xn[:, q, :], 0).then_inc(S("ln1_done"), 1)
                if isinstance(b, int) and b == 0:
                    gelu(1)
                if isinstance(b, int) and b == NB + 1:
                    shared_gate(0)
                    shared_mul(0)
                if isinstance(b, int) and b == NB + 2:
                    shared_out(0)

            for n in range(2):
                mix(n, 0)
                for g in range(1, NG):
                    mix(n, g)
                dve.wait_ge(S("mix_chain"), NG)
                nc.vector.bn_stats(st[:, n, :], image(h_all, n)).then_inc(S("ln_chain"), 1)
            for n in range(2):
                dve.wait_ge(S("ln_chain"), 2)
                nc.vector.bn_aggr(mv[:, n, :], st[:, n, :]).then_inc(S("ln_chain"), 1)
            for k in range(ROOT + 1):
                root(k, 0, 2, 4)
            for n in range(2):
                dve.wait_ge(S("ln_chain"), 4 + ROOT + 1)
                apply(image(h_all, n), xn[:, n, :], n).then_inc(S("ln1_done"), 1)
            image_loop(dve, step, -1, NB + 2)

            tn = [0]

            def lt(ins):
                link(ins, "t_chain", 0, tn)
            dve.wait_ge(S("t_count"), 1)
            lt(nc.vector.tensor_scalar(cnt_i[:, 0:1], psX[0:E, 0:1], float(P - 1), None, ALU.add))
            lt(nc.vector.tensor_single_scalar(cnt_i[:, 1:2], cnt_i[:, 0:1], 7, ALU.arith_shift_right))
            lt(nc.vector.tensor_copy(nt_f[:, 1:2], cnt_i[:, 1:2]))
            nc.vector.tensor_scalar(nt_f[:, 2:3], nt_f[:, 1:2], 0.0, None, ALU.is_gt)
            lt(nc.vector.scalar_tensor_tensor(out=tab[:, 0, 0:E], in0=psX[0:1, E:2 * E], scalar=-1.0,
                                              in1=c("ebase", 1), op0=ALU.add, op1=ALU.add))
            nc.vector.tensor_copy(pad_ix[:], tab[:, 0, 0:E]).then_inc(S("pad_ready"), 1)
            nc.vector.tensor_copy(nt_b[:], nt_f[:, 1:2]).then_inc(S("t_rows"), 1)
            dve.wait_ge(S("t_cum"), 1)
            lt(nc.vector.tensor_copy(cum[:], psX[0:E, 0:1]))
            nc.vector.tensor_scalar(past[:], c("tile", E), cum[:, 0:1], None, ALU.is_ge).then_inc(S("t_rows"), 1)
            dve.wait_ge(S("t_past"), 1)
            ex, before, rank = (psX[0:1, k * NTAB:(k + 1) * NTAB] for k in range(3))
            lt(nc.vector.tensor_tensor(tab[:, 1, :], c("tile", 1), before, ALU.subtract))
            lt(nc.vector.tensor_scalar(tab[:, 1, :], tab[:, 1, :], float(P), None, ALU.mult))
            lt(nc.vector.scalar_tensor_tensor(out=tab[:, 2, :], in0=ex, scalar=float(REGION), in1=tab[:, 1, :],
                                              op0=ALU.mult, op1=ALU.add))
            nc.vector.tensor_scalar(tab[:, 3, :], tab[:, 2, :], float(SLOTS), None, ALU.min).then_inc(
                S("t_rowf"), 1)
            dve.wait_ge(S("t_rowf"), 1)
            nc.vector.tensor_copy(tab_i[:, :, 0], tab[:, 3, :]).then_inc(S("tab_ready"), 1)
            nc.vector.tensor_scalar(tab_i[:, :, 2], ex, float(E - 1), None, ALU.min).then_inc(S("tab_ready"), 1)
            lt(nc.vector.tensor_copy(rank_i[:], rank))
            lt(nc.vector.tensor_copy(tabf[:, 1:NTAB + 1], rank))
            nc.vector.tensor_single_scalar(tab_i[:, :, 1], rank_i[:], RING - 1, ALU.bitwise_and)
            lt(nc.vector.tensor_single_scalar(slot_i[:, 2:NTAB + 2], rank_i[:], RING - 1, ALU.bitwise_and))
            nc.vector.tensor_tensor(tab_i[:, :, 3], tabf[:, 1:NTAB + 1], tabf[:, 0:NTAB],
                                    ALU.not_equal).then_inc(S("tab_ready"), 1)
            lt(nc.vector.tensor_scalar(live[:], psX[0:1, 0:NTAB:U][:, 0:TURNS + 1], float(E), None, ALU.is_lt))
            lt(nc.vector.reduce_sum(live[:, 0:1], live[:, 0:TURNS], axis=AX))
            nc.vector.tensor_scalar(last_turn[:], live[:, 0:1], -1.0, None, ALU.add).then_inc(S("tab_ready"), 1)
            nc.vector.tensor_copy(turn_slots[:, :, 0:U],
                                  slot_i[:, 0:(TURNS + 1) * U].rearrange("p (t u) -> p t u", u=U))
            nc.vector.tensor_copy(turn_slots[:, 0:TURNS, U:U + 2],
                                  slot_i[:, U:(TURNS + 1) * U].rearrange("p (t u) -> p t u", u=U)[:, :, 0:2]
                                  ).then_inc(S("tab_ready"), 1)
            dve.wait_ge(S("t_bcast"), 1)
            nc.vector.tensor_scalar(myslot[:], psC[:, 0:NTAB], c("part"), None, ALU.add).then_inc(
                S("myslot_ready"), 1)
            dve.wait_ge(S("myslot_ready"), 1)
            dve.wait_ge(S("tab_ready"), TABLES)

            for j in range(1, 4):
                shared_gate(j)
                shared_mul(j)
                shared_out(j)

            def tile_step(i, q, t, tail):
                if not tail:
                    dve.wait_ge(xt_in[q], 16 * i + 16)
                    wait(dve, S("y_ready"), t - U + 1)
                    nc.vector.tensor_copy(token_ix[:, q, :], xring[:, q, ID_AT:ID_AT + 1].bitcast(I32))
                    nc.vector.scalar_tensor_tensor(
                        out=wtj[:, q, :], in0=xring[:, q, S_AT:S_AT + TOPK], scalar=myslot[:, ds(t, 1)],
                        in1=xring[:, q, W_AT:W_AT + TOPK], op0=ALU.is_equal, op1=ALU.mult,
                        accum_out=wtile[:, q, :]).then_inc(S("wt_done"), 1)
                    dve.wait_ge(S("silu_done"), t + 1)
                    wait(dve, S("h_turned"), t - 1)
                    nc.vector.tensor_tensor(hm[:, q % 2, :], silu[:, q % 2, :], psS[q % 2][:, INTER:2 * INTER],
                                            ALU.mult).then_inc(S("h_ready"), 1)
                v, a = t - 2, (q - 2) % NACC
                if has(v, 0, NT):
                    dve.wait_ge(S("down_done"), t - 1)
                    dve.wait_ge(S("wt_done"), t - 1)
                    turn = U // NACC * i + (q - 2) // NACC
                    wait(dve, added[a], 16 * turn)
                    nc.vector.tensor_scalar(y[:, a, :], ps[6 + q % 2][:, 0:D], wtile[:, (q - 2) % U, :], None,
                                            ALU.mult).then_inc(S("y_ready"), 1)
            tile_loop(dve, VECTOR, tile_step, 0, 2)

            for j in range(NCH):
                dve.wait_ge(fin_in[j], 16 * NACC)
                f = [fin_sb[:, j, a, :] for a in range(NACC)]
                rest = h_all[:, FIN * j:FIN * j + FIN, :].rearrange("p b d -> p (b d)")
                dve.wait_ge(S("h2_ready"), FIN * (j + 1))
                nc.vector.tensor_tensor(f[0], f[0], f[1], ALU.add).then_inc(S("fin_chain"), 1)
                nc.vector.tensor_tensor(f[2], f[2], rest, ALU.add).then_inc(S("fin_chain"), 1)
                dve.wait_ge(S("fin_chain"), 2 * j + 2)
                nc.vector.tensor_tensor(f[0], f[0], f[2], ALU.add).then_inc(S("fin_ready"), 1)

        @block.tensor
        def _(pe):
            def mm(*a, **k):
                return nc.tensor.matmul(*a, **k)

            def both(dst, lhs, rhs):
                for k in range(KT):
                    last = mm(dst, lhs(k), rhs(k), start=k == 0, stop=k == KT - 1)
                return last

            def mixing_in(part):
                lo, hi = PARTS[part]
                n, at = hi - lo, psC if part else psA
                pe.wait_ge(weights_in[0], 16)
                for name, sums in (("sum_act", ACT_SUMS), ("sum_dve", DVE_SUMS)):
                    pe.wait_ge(S(name), sum(img < hi for part_of in sums.values() for img in part_of))
                mm(at[0:HID, 0:n], w1_sb[:], xsum[:, lo:hi], start=True, stop=True).then_inc(S("tok_h"), 1)

            def mixing_out(part):
                lo, hi = PARTS[part]
                n, at = hi - lo, psC if part else psA
                pe.wait_ge(weights_in[2], 16)
                pe.wait_ge(S("tok_hid"), 2 * part + 2)
                for g in range(NG):
                    last = mm(at[:, g * n:(g + 1) * n], w2_sb[:, g, :], gel[:, 4, lo:hi], start=True, stop=True)
                last.then_inc(S("tok_w"), 1)

            mixing_in(0)
            mixing_out(0)
            pe.wait_ge(weights_in[4], 16)
            pe.wait_ge(S("consts_ready"), 1)

            def shared_up(j, m):
                if j:
                    if m < 2:
                        pe.wait_ge(S("sh_mul"), 2 * (j - 1) + m + 1)
                    else:
                        pe.wait_ge(S("sh_chain"), 2 * (j - 1) + m - 1)
                pe.wait_ge(S("x2t_ready"), 8 * j + 8)
                x4 = x_sb[:, 4 * j:4 * j + 4, 1, :]
                both((psG + psU)[m][:], lambda k: sgu_sb[:, k, m * P:(m + 1) * P],
                     lambda k: x4[:, :, k * P:(k + 1) * P]).then_inc(S("gu_done"), 1)

            def shared_down(j):
                pe.wait_ge(S("sh_chain"), 2 * j + 2)
                for n in range(4):
                    wait(pe, S("h2_ready"), 4 * j + n - 1)
                    both(psD[n % 2][:, 0:D], lambda k: sht[:, j % 2, k, n * P:(n + 1) * P],
                         lambda k: sd_sb[:, k, :]).then_inc(S("shared_done"), 1)

            FIRST_CHUNK = {(NB, 1): 0, (NB, 3): 1, (NB + 1, 1): 2, (NB + 1, 2): 3, (NB + 2, 1): 4}

            def shared_between(b, k):
                part = FIRST_CHUNK.get((b, k)) if isinstance(b, int) else None
                if part == 4:
                    shared_down(0)
                elif part is not None:
                    shared_up(0, part)

            def step(b, par):
                a, v, cc, d, e, q = b + 2, b + 1, b - 1, b - 2, b - 3, 1 - par
                if isinstance(b, int) and b == 0:
                    for k in (7, 10, 11, 12):
                        pe.wait_ge(weights_in[k], 16)

                def scores(img, g, p):
                    n, sp = NGRP * img + g, g % 2
                    if g % 2 == 0:
                        pe.wait_ge(S("kmask_ready"), 2 * img + g // 2 + 1)
                        pe.wait_ge(S("q_ready"), 2 * img + 2)
                    wait(pe, S("exp_done"), n - 1)
                    mm(psS[sp][:], ident_b[:], causal_b[:].rearrange("p a k -> p (a k)"), start=True, stop=False)
                    mm(psS[sp][:], qt[:, p, g // 2, :],
                       kmask[:, p, GH * g:GH * g + GH, :].rearrange("p a k -> p (a k)"),
                       start=False, stop=True).then_inc(S("scores_done"), 1)

                def turn(g):
                    n, sp = NGRP * b + g, g % 2
                    pe.wait_ge(S("exp_done"), n + 1)
                    wait(pe, S("probt_ready"), n - 1)
                    for j in range(GH):
                        last = nc.tensor.transpose(psT[sp][:, j * P:(j + 1) * P], prob[:, sp, j, :], ident)
                    last.then_inc(S("prob_transposed"), 1)

                def pv(g):
                    n, sp = NGRP * b + g, g % 2
                    pe.wait_ge(S("probt_ready"), n + 1)
                    if g == 0:
                        pe.wait_ge(S("v_ready"), b + 1)
                        wait(pe, S("ot_ready"), b)
                    for j in range(GH):
                        last = mm(psO[32 * j:32 * j + 32, g * P:(g + 1) * P], vaug[:, par, GH * g + j, :],
                                  probt[:, sp, j, :], start=True, stop=True)
                    last.then_inc(S("pv_done"), 1)

                def two(dst, src, done):
                    for k in range(KT):
                        last = nc.tensor.transpose(dst[:, k * P:(k + 1) * P], src[:, k * P:(k + 1) * P], ident)
                    last.then_inc(S(done), 1)

                def project(which):
                    for m in which:
                        last = both(psA[:, m * P:(m + 1) * P], lambda k: wqkv_sb[:, k, m * P:(m + 1) * P],
                                    lambda k: xnt[:, par, k, :])
                    last.then_inc(S("qk_done"), 1)

                if has(e):
                    pe.wait_ge(S("sel_ready"), e + 1)
                    mm(psC[:, 0:E], before_b[:], sel_b[:, q, :], start=True, stop=False)
                    mm(psC[:, 0:E], ones_b[:], selsum[:], start=False, stop=True).then_inc(S("pos_done"), 1)
                if has(b):
                    turn(0)
                if has(cc):
                    pe.wait_ge(S("ot_ready"), cc + 1)
                    wait(pe, S("gate_tanh"), cc - 1)
                    for g in range(NGRP):
                        last = nc.tensor.transpose(psX[:, g * P:(g + 1) * P], ot_sb[:, g, :], ident)
                    last.then_inc(S("ot_turned"), 1)
                if has(b):
                    scores(b, 2, par)
                    pv(0)
                if has(v):
                    wait(pe, S("q_ready"), 2 * v + 2)
                    both(psA[:, 0:D], lambda k: xnt[:, q, k, :], lambda k: wqkv_sb[:, k, 2 * D:3 * D]).then_inc(
                        S("v_done"), 1)
                if has(d):
                    pe.wait_ge(S("x2_ready"), d + 1)
                    wait(pe, S("o_ready"), cc + 1 if not isinstance(cc, int) else min(cc + 1, NB))
                    two(psX, row[:, par, :], "x2_transposed")
                shared_between(b, 0)
                if has(b):
                    turn(1)
                    scores(b, 3, par)
                if has(cc):
                    pe.wait_ge(S("o_ready"), cc + 1)
                    wait(pe, S("key_read"), e + 1)
                    two(psC, o_sb, "o_transposed")
                if has(b):
                    pv(1)
                if has(a):
                    pe.wait_ge(S("ln1_done"), a + 1)
                    wait(pe, S("v_ready"), a)
                    two(psA, xn[:, par, :], "xn_transposed")
                if has(d):
                    pe.wait_ge(S("x2t_ready"), 2 * d + 2)
                    both(psX[:, 0:E], lambda k: x2t[:, k, :], lambda k: gate_sb[:, k, :]).then_inc(
                        S("gate_done"), 1)
                shared_between(b, 1)
                if has(b):
                    turn(2)
                if has(v):
                    scores(v, 0, q)
                if has(b):
                    pv(2)
                if isinstance(b, int) and b == 0:
                    mixing_in(1)
                if has(cc):
                    pe.wait_ge(S("ont_ready"), cc + 1)
                    wait(pe, S("x2_ready"), cc)
                    both(psC[:, D:2 * D], lambda k: ont[:, k, :], lambda k: wo_sb[:, k, :]).then_inc(
                        S("proj_done"), 1)
                if has(a):
                    pe.wait_ge(S("xnt_ready"), a + 1)
                    project((2, 3))
                shared_between(b, 2)
                if has(b):
                    turn(3)
                if has(v):
                    scores(v, 1, q)
                if has(b):
                    pv(3)
                if has(a):
                    pe.wait_ge(S("k_ready"), 2 * a + 2)
                    project((0, 1))
                shared_between(b, 3)
                if isinstance(b, int) and b == 0:
                    mixing_out(1)
            image_loop(pe, step, -2, NB + 2)

            pe.wait_ge(S("row_ready"), NB)
            mm(psX[0:E, 0:1], selsum[:], ones_b[:, 0:1], start=True, stop=True)
            mm(psX[0:1, E:2 * E], ones_b[:, 0:1], selsum[:], start=True, stop=True).then_inc(S("t_count"), 1)
            shared_up(1, 0)
            pe.wait_ge(S("t_rows"), 1)
            mm(psX[0:E, 0:1], upto_b[:], nt_b[:], start=True, stop=True).then_inc(S("t_cum"), 1)
            shared_up(1, 1)
            pe.wait_ge(S("t_rows"), 2)
            for k in range(3):
                last = mm(psX[0:1, k * NTAB:(k + 1) * NTAB], nt_f[:, k:k + 1], past[:], start=True, stop=True)
            last.then_inc(S("t_past"), 1)
            shared_up(1, 2)
            shared_up(1, 3)
            pe.wait_ge(S("t_rowf"), 1)
            mm(psC[:, 0:NTAB], ones_f[0:1, :], tab[:, 3, :], start=True, stop=True).then_inc(S("t_bcast"), 1)
            for j in range(1, 4):
                for m in range(4):
                    if m == 2:
                        shared_down(j)
                    if j < 3:
                        shared_up(j + 1, m)
            pe.wait_ge(S("tab_ready"), TABLES)
            pe.wait_ge(S("myslot_ready"), 1)
            pe.wait_ge(S("h2_ready"), 16)

            slots = []

            def tile_step(i, q, t, tail):
                u = t + 1
                if q <= 0:
                    row8 = turn_slots[0:1, ds(i, 1), :].rearrange("p a b -> p (a b)")
                    slots[:] = loaded(row8, PE, (RING - 1,) * SLOTS_AT)
                if not tail:
                    uq = (q + 1) % U
                    pe.wait_ge(xt_in[uq], 16 * (i + (q + 1) // U) + 16)
                    wait(pe, S("xt_ready"), u - 1)
                    for k in range(KT):
                        last = nc.tensor.transpose(psT[uq % 2][:, k * P:(k + 1) * P],
                                                   xring[:, uq, k * P:(k + 1) * P], ident)
                    last.then_inc(S("xt_done"), 1)
                if has(t, 0, NT) and not tail:
                    pe.wait_ge(S("xt_ready"), t + 1)
                    pe.wait_ge(w_in[q], 16 * i + 16)
                    wait(pe, S("h_ready"), t - 1)
                    both(psS[q % 2][:, 0:2 * INTER], lambda k: xt[:, q % 2, k, :],
                         lambda k: wring[:, ds(slots[q + 2], 1), k * 2 * INTER:(k + 1) * 2 * INTER]).then_inc(
                        S("up_done"), 1)
                v = t - 1
                if has(v, 0, NT) and not (tail and q):
                    vq = (q - 1) % 2
                    pe.wait_ge(S("h_ready"), v + 1)
                    wait(pe, S("ht_ready"), v - 1)
                    nc.tensor.transpose(ps[4 + vq][:, 0:P], hm[:, vq, :], ident).then_inc(S("h_turned"), 1)
                v = t - 2
                if has(v, 0, NT):
                    vq = q % 2
                    pe.wait_ge(S("ht_ready"), v + 1)
                    wait(pe, S("y_ready"), v - 1)
                    mm(ps[6 + vq][:, 0:D], ht[:, vq, :], wring[:, ds(slots[q], 1), KT * 2 * INTER:WCOLS],
                       start=True, stop=True).then_inc(S("down_done"), 1)
            tile_loop(pe, PE, tile_step, -1, 2)


_ARGS = ("x", "w1t", "b1", "w2t", "b2", "wqkv", "bqk", "bv", "wo", "bo", "gate", "gbias", "sgu", "sd", "wexp",
         "const")


def kernel(x, L0_tok_w1, L0_tok_b1, L0_tok_w2, L0_tok_b2, L0_attn_W_qkv, L0_attn_b_qkv, L0_attn_W_o, L0_attn_b_o,
           L0_ffn_gate_w, L0_ffn_gate_bias, L0_ffn_eg_w, L0_ffn_eu_w, L0_ffn_ed_w, L0_ffn_sg_w, L0_ffn_su_w,
           L0_ffn_sd_w):
    import numpy as np
    import concourse.bacc as bacc
    from concourse.bass_utils import run_bass_kernel_spmd

    def rows(w):
        w = np.asarray(w)
        return np.ascontiguousarray(w.T.reshape(KT, P, w.shape[0]).transpose(1, 0, 2))

    const = np.zeros((P, C_COLS), np.float32)

    def put(name, v):
        at, n = C_AT[name]
        const[:, at:at + n] = v
    p = np.arange(P)
    put("ident", np.eye(P))
    put("causal", np.where(p[None, :] > p[:, None], NEG, 0.0))
    put("before", p[:, None] < p[None, :])
    put("head", p[:, None] // HD == np.arange(8)[None, :])
    put("ebase", np.arange(E)[None, :] * REGION + 1)
    put("ids", (np.arange(NB)[None, :] * P + p[:, None]).astype(np.int32).view(np.float32))
    pad = np.zeros((P, ROW), np.float32)
    pad[:, S_AT:S_AT + TOPK] = -1.0
    pad[:, ID_AT] = (TOKENS + p).astype(np.int32).view(np.float32)
    put("pad", pad)
    put("upto", p[:, None] <= np.arange(E)[None, :])
    put("tile", np.arange(NTAB)[None, :])
    put("part", p[:, None])

    eg, eu, ed = (np.asarray(w) for w in (L0_ffn_eg_w, L0_ffn_eu_w, L0_ffn_ed_w))
    up = np.stack([eg, eu], 1).reshape(E, 2 * INTER, KT, P).transpose(0, 3, 2, 1).reshape(E, P, KT * 2 * INTER)
    wexp = np.ascontiguousarray(np.concatenate([up, ed.transpose(0, 2, 1)], 2))
    bqkv = np.asarray(L0_attn_b_qkv)
    arrays = dict(
        x=np.asarray(x), w1t=np.ascontiguousarray(np.asarray(L0_tok_w1).T), b1=np.asarray(L0_tok_b1)[:, None],
        w2t=np.ascontiguousarray(np.asarray(L0_tok_w2).reshape(P, NG, HID).transpose(2, 1, 0)),
        b2=np.asarray(L0_tok_b2).reshape(P, NG), wqkv=rows(L0_attn_W_qkv),
        bqk=np.ascontiguousarray(bqkv[:2 * D].reshape(4, P).T), bv=bqkv[2 * D:][None, :], wo=rows(L0_attn_W_o),
        bo=np.asarray(L0_attn_b_o)[None, :], gate=rows(L0_ffn_gate_w), gbias=np.asarray(L0_ffn_gate_bias)[None, :],
        sgu=rows(np.concatenate([np.asarray(L0_ffn_sg_w), np.asarray(L0_ffn_su_w)], 0)), sd=rows(L0_ffn_sd_w),
        wexp=wexp, const=const)
    arrays = {k: np.ascontiguousarray(v) for k, v in arrays.items()}

    nc = bacc.Bacc("TRN2", target_bir_lowering=False, num_devices=1)
    aps = [nc.dram_tensor(n, arrays[n].shape, mybir.dt.from_np(arrays[n].dtype), kind="ExternalInput").ap()
           for n in _ARGS]
    out = nc.dram_tensor("out", (TOKENS, D), F32, kind="ExternalOutput").ap()
    build(nc, *aps, out)
    r = run_bass_kernel_spmd(nc, [arrays], core_ids=[0])
    return np.asarray(r.results[0]["out"]).reshape(NB, P, D)
```
